# Optimizing a Trainium2 kernel written in Bass

```python
import numpy as np
import jax
import jax.numpy as jnp

def _softmax(x, axis=-1):
    return jax.nn.softmax(x, axis=axis)

def _gelu(x):
    return jax.nn.gelu(x, approximate=True)

def _silu(x):
    return jax.nn.silu(x)

def _sigmoid(x):
    return jax.nn.sigmoid(x)

def _layernorm(x, axis=-1, eps=1e-05):
    m = jnp.mean(x, axis=axis, keepdims=True)
    v = jnp.var(x, axis=axis, keepdims=True)
    return (x - m) / jnp.sqrt(v + eps)

def _scatter_add(tgt, idx, src, axis=0):
    return tgt.at[idx].add(src)

def _segment_sum(src, seg, n):
    return jax.ops.segment_sum(src, seg, n)
kernel_name = 'mk_adj_resnorm_d1_adj_r2_11efc2'

def setup_inputs(seed: int=0):
    np.random.seed(seed)
    _w = jnp.asarray

    def _rec_inputs():
        import jax
        import jax.numpy as jnp
        _gk = jax.random.key(seed)
        x = -0.0005207 + 1.001 * jax.random.normal(jax.random.fold_in(_gk, 1), (4096, 256), jnp.float32)
        _w = (1.0 + jnp.arange(4096, dtype=jnp.float32)) ** (-0.5)
        _w = _w / _w.mean()
        _pij = jnp.clip(0.00195312 * _w[:, None] * _w[None, :], 0.0, 1.0)
        _a = jax.random.uniform(jax.random.fold_in(_gk, 2), (4096, 4096)) < _pij
        _af = _a.astype(jnp.float32)
        adj = _af
        return (x, adj)
    x, adj = _rec_inputs()

    def _L0_gnn_setup():
        import jax, jax.numpy as jnp
        import numpy as np
        N = 2048
        INPUT_DIM = 256
        KEY_DIM = 64
        OUT_DIM = 256
        N_HEADS = 8

        def _xavier_normal(key, shape, gain):
            fan_in, fan_out = (shape[-2], shape[-1])
            std = gain * (2.0 / (fan_in + fan_out)) ** 0.5
            return jax.random.normal(key, shape, dtype=jnp.float32) * std
        key = jax.random.key(seed)
        kx, ka, kk, kq, kv, ko = jax.random.split(key, 6)
        gain = 2.0 ** 0.5
        node_matrix = jax.random.normal(kx, (N, INPUT_DIM), dtype=jnp.float32)
        adjacency_matrix = jax.random.randint(ka, (N, N), 0, 2).astype(jnp.float32)
        Wks = _xavier_normal(kk, (N_HEADS, INPUT_DIM, KEY_DIM), gain)
        Wqs = _xavier_normal(kq, (N_HEADS, INPUT_DIM, KEY_DIM), gain)
        Wvs = _xavier_normal(kv, (N_HEADS, INPUT_DIM, KEY_DIM), gain)
        Wo = _xavier_normal(ko, (N_HEADS, KEY_DIM, OUT_DIM), gain)
        return {'node_matrix': node_matrix, 'adjacency_matrix': adjacency_matrix, 'Wks': Wks, 'Wqs': Wqs, 'Wvs': Wvs, 'Wo': Wo}
    _L0_gnn_all = _L0_gnn_setup()
    _L0_gnn_in = {k: v for k, v in _L0_gnn_all.items() if k in ('Wks', 'Wqs', 'Wvs', 'Wo')}
    del _L0_gnn_all
    return {'x': x, 'adj': adj, 'L0_gnn_Wks': _L0_gnn_in['Wks'], 'L0_gnn_Wqs': _L0_gnn_in['Wqs'], 'L0_gnn_Wvs': _L0_gnn_in['Wvs'], 'L0_gnn_Wo': _L0_gnn_in['Wo']}

def reference(x, adj, L0_gnn_Wks, L0_gnn_Wqs, L0_gnn_Wvs, L0_gnn_Wo):
    import jax
    import jax.numpy as jnp

    def _L0_gnn_ref(node_matrix, adjacency_matrix, Wks, Wqs, Wvs, Wo):
        import jax, jax.numpy as jnp
        import numpy as np
        N = 2048
        INPUT_DIM = 256
        KEY_DIM = 64
        OUT_DIM = 256
        N_HEADS = 8

        def _xavier_normal(key, shape, gain):
            fan_in, fan_out = (shape[-2], shape[-1])
            std = gain * (2.0 / (fan_in + fan_out)) ** 0.5
            return jax.random.normal(key, shape, dtype=jnp.float32) * std
        n = adjacency_matrix.shape[0]
        adj = jnp.maximum(adjacency_matrix, jnp.eye(n, dtype=adjacency_matrix.dtype))
        keys = jnp.einsum('nj,hjk->hnk', node_matrix, Wks)
        queries = jnp.einsum('nj,hjk->hnk', node_matrix, Wqs)
        values = jnp.einsum('nj,hjk->hnk', node_matrix, Wvs)
        key_dim = Wks.shape[-1]
        atts = jnp.einsum('hqk,hmk->hqm', queries, keys) / key_dim ** 0.5
        atts = atts - 1e+16 * (1.0 - adj)[None, :, :]
        atts = jax.nn.softmax(atts, axis=-1)
        return jnp.einsum('hqm,hmk,hko->qo', atts, values, Wo)
    x = _layernorm(x + _L0_gnn_ref(x, adj, L0_gnn_Wks, L0_gnn_Wqs, L0_gnn_Wvs, L0_gnn_Wo), axis=-1)
    return x

_drawn_inputs = setup_inputs


def setup_inputs(seed=0):
    import zlib

    import numpy as np

    out = dict(_drawn_inputs(seed))
    spreads = {}
    factors = {}
    for name, (base, spread) in spreads.items():
        noise = np.random.default_rng([zlib.crc32(name.encode()), seed]).standard_normal(out[name].shape)
        drawn = base * np.exp(spread * noise) if base else spread * noise
        out[name] = jnp.asarray(drawn.astype(out[name].dtype))
    for name, factor in factors.items():
        out[name] = (out[name] * factor).astype(out[name].dtype)
    return out
```

```python
from contextlib import ExitStack

import concourse.bass as bass
from concourse import mybir

ALU = mybir.AluOpType
ACT = mybir.ActivationFunctionType
AX = mybir.AxisListType
F32 = mybir.dt.float32
F32R = mybir.dt.float32r
BF16 = mybir.dt.bfloat16

P = 128
BANK = 512
BIG = 1e16
EPS = 1e-5


def due(n):
    return not isinstance(n, int) or n > 0


def projections(nc, x, wk, wq, wv, q_scr, k_scr, v_scr):
    N, D = x.shape
    H, _, DK = wk.shape
    CD = D // P
    CB = BANK // P
    CHUNKS = N // BANK
    PAIRS = H // 2
    TILES = 2 * PAIRS
    RING = 4
    with ExitStack() as ctx:
        def sb(name, shape, dt=F32):
            return ctx.enter_context(nc.sbuf_tensor(name, shape, dt))

        def sem(name):
            return ctx.enter_context(nc.semaphore(name))

        ident = sb("p_ident", [P, P])
        w_sb = [sb("wk_sb", [P, CD, H * DK]), sb("wq_sb", [P, CD, H * DK])]
        wv_sb = sb("wv_sb", [P, CD, H * DK])
        xin = [sb(f"xin{u}", [P, CB, D]) for u in range(2)]
        xT = [sb(f"xT{u}", [P, CD, BANK]) for u in range(2)]
        high = [sb(f"high{s}", [P, BANK], F32R) for s in range(RING)]
        low = [sb(f"low{s}", [P, BANK], F32R) for s in range(RING)]
        v_all = sb("v_all", [P, H, N // P, DK])
        ps_x = [ctx.enter_context(nc.psum_tensor(f"ps_x{c}", [P, BANK], F32)) for c in range(CD)]
        ps_p = [ctx.enter_context(nc.psum_tensor(f"ps_p{s}", [P, BANK], F32)) for s in range(4)]
        ps_v = [ctx.enter_context(nc.psum_tensor(f"ps_v{s}", [P, BANK], F32)) for s in range(2)]

        weights_in = sem("weights_in")
        x_in = [sem(f"x_in{u}") for u in range(2)]
        ident_zero = sem("p_ident_zero")
        ident_done = sem("p_ident_done")
        x_turned = sem("x_turned")
        xT_act = sem("xT_act")
        xT_dve = sem("xT_dve")
        projected = sem("projected")
        high_done = sem("high_done")
        low_done = sem("low_done")
        stored = [sem(f"stored{s}") for s in range(RING)]
        v_made = sem("v_made")
        v_act = sem("v_act")
        v_dve = sem("v_dve")
        v_stored = sem("v_stored")

        block = ctx.enter_context(nc.Block())

        @block.gpsimd
        def _(pool):
            nc.gpsimd.memset(ident[:], 0.0).then_inc(ident_zero, 1)
            pool.wait_ge(ident_zero, 1)
            nc.gpsimd.affine_select(out=ident[:], in_=ident[:], compare_op=ALU.not_equal, fill=1.0,
                                    base=0, pattern=[[-1, P]], channel_multiplier=1).then_inc(ident_done, 1)
            xd = x.rearrange("(n b p) d -> n p b d", p=P, b=CB)
            for u in range(2):
                pool.dma_start(xin[u][:], xd[u]).then_inc(x_in[u], 16)
            with pool.Fori(1, CHUNKS // 2) as r:
                for u in range(2):
                    pool.wait_ge(x_turned, 2 * r + (u - 1))
                    pool.dma_start(xin[u][:], xd[2 * r + u]).then_inc(x_in[u], 16)

        @block.sync
        def _(sp):
            for w, t in ((wk, w_sb[0]), (wq, w_sb[1]), (wv, wv_sb)):
                for c in range(CD):
                    sp.dma_start(t[:, c, :].rearrange("p (h k) -> p h k", h=H),
                                 w[:, c * P:(c + 1) * P, :].rearrange("h p k -> p h k")).then_inc(weights_in, 16)
            with sp.Fori(0, CHUNKS) as n:
                for t in range(TILES):
                    s, pair, scr = t % RING, t // 2, (k_scr, q_scr)[t % 2]
                    sp.wait_ge(high_done, n * TILES + (t + 1))
                    for hh in range(2):
                        sp.dma_start(scr[2 * pair + hh, 0, :, bass.ts(n, BANK)],
                                     high[s][hh * DK:(hh + 1) * DK, :].bitcast(F32)).then_inc(stored[s], 16)
                    sp.wait_ge(low_done, n * TILES + (t + 1))
                    for hh in range(2):
                        sp.dma_start(scr[2 * pair + hh, 1, :, bass.ts(n, BANK)],
                                     low[s][hh * DK:(hh + 1) * DK, :].bitcast(F32)).then_inc(stored[s], 16)
            sp.wait_ge(v_act, CHUNKS * CB // 2)
            sp.wait_ge(v_dve, CHUNKS * CB // 2)
            for h in range(H):
                sp.dma_start(v_scr[h], v_all[:, h]).then_inc(v_stored, 16)
            sp.wait_ge(v_stored, 16 * H)
            for s in range(RING):
                sp.wait_ge(stored[s], 64 * CHUNKS * TILES // RING)

        @block.tensor
        def _(pe):
            pe.wait_ge(ident_done, 1)

            def chunk(r, u, first):
                n = 2 * r + u
                pe.wait_ge(x_in[u], 16 * r + 16)
                if not first:
                    pe.wait_ge(xT_act, n)
                    pe.wait_ge(xT_dve, n)
                for c in range(CD):
                    for b in range(CB):
                        last = nc.tensor.transpose(ps_x[c][:, b * P:(b + 1) * P],
                                                   xin[u][:, b, c * P:(c + 1) * P], ident[:])
                last.then_inc(x_turned, 1)
                if first:
                    pe.wait_ge(weights_in, 16 * 3 * CD)
                pe.wait_ge(xT_act, n + 1)
                pe.wait_ge(xT_dve, n + 1)
                for t in range(TILES):
                    w = w_sb[t % 2]
                    pair = t // 2
                    if not first or t >= 4:
                        pe.wait_ge(low_done, n * TILES + (t - 3))
                    for c in range(CD):
                        last = nc.tensor.matmul(ps_p[t % 4][:], w[:, c, pair * P:(pair + 1) * P],
                                                xT[u][:, c, :], start=(c == 0), stop=(c == CD - 1))
                    last.then_inc(projected, 1)
                for b in range(CB):
                    if not first or b >= 2:
                        pe.wait_ge((v_act, v_dve)[b % 2], n * (CB // 2) + b // 2)
                    for c in range(CD):
                        last = nc.tensor.matmul(ps_v[b % 2][:], xT[u][:, c, b * P:(b + 1) * P],
                                                wv_sb[:, c, :], start=(c == 0), stop=(c == CD - 1))
                    last.then_inc(v_made, 1)

            chunk(0, 0, True)
            chunk(0, 1, False)
            with pe.Fori(1, CHUNKS // 2) as r:
                chunk(r, 0, False)
                chunk(r, 1, False)

        def v_slot(n, b):
            return v_all[:, :, bass.ds(n * CB + b, 1), :].rearrange("p h o k -> p h (o k)")

        @block.scalar
        def _(act):
            def chunk(r, u, first):
                n = 2 * r + u
                act.wait_ge(x_turned, n + 1)
                if not first:
                    act.wait_ge(v_made, (n - 1) * CB)
                nc.scalar.copy(xT[u][:, 0, :], ps_x[0][:]).then_inc(xT_act, 1)
                for t in range(TILES):
                    act.wait_ge(projected, n * TILES + (t + 1))
                    if not first or t >= RING:
                        act.wait_ge(stored[t % RING], 64 * ((TILES // RING) * n + t // RING))
                    nc.scalar.activation(high[t % RING][:], ps_p[t % 4][:], ACT.Copy,
                                         scale=(1.0, -(DK ** -0.5))[t % 2]).then_inc(high_done, 1)
                for b in range(0, CB, 2):
                    act.wait_ge(v_made, n * CB + (b + 1))
                    nc.scalar.copy(v_slot(n, b), ps_v[0][:].rearrange("p (h k) -> p h k", h=H)).then_inc(v_act, 1)

            chunk(0, 0, True)
            chunk(0, 1, False)
            with act.Fori(1, CHUNKS // 2) as r:
                chunk(r, 0, False)
                chunk(r, 1, False)

        @block.vector
        def _(dve):
            def chunk(r, u, first):
                n = 2 * r + u
                dve.wait_ge(x_turned, n + 1)
                if not first:
                    dve.wait_ge(v_made, (n - 1) * CB)
                nc.vector.tensor_copy(xT[u][:, 1, :], ps_x[1][:]).then_inc(xT_dve, 1)
                for t in range(TILES):
                    dve.wait_ge(high_done, n * TILES + (t + 1))
                    if not first or t >= RING:
                        dve.wait_ge(stored[t % RING], 64 * ((TILES // RING) * n + t // RING))
                    nc.vector.scalar_tensor_tensor(out=low[t % RING][:], in0=ps_p[t % 4][:],
                                                   scalar=(1.0, -(DK ** -0.5))[t % 2],
                                                   in1=high[t % RING][:].bitcast(F32),
                                                   op0=ALU.mult, op1=ALU.subtract).then_inc(low_done, 1)
                for b in range(1, CB, 2):
                    dve.wait_ge(v_made, n * CB + (b + 1))
                    nc.vector.tensor_copy(v_slot(n, b), ps_v[1][:].rearrange("p (h k) -> p h k", h=H)).then_inc(v_dve, 1)

            chunk(0, 0, True)
            chunk(0, 1, False)
            with dve.Fori(1, CHUNKS // 2) as r:
                chunk(r, 0, False)
                chunk(r, 1, False)


def attention(nc, adj, wo, q_scr, k_scr, v_scr, y_scr):
    H, _, DK, N = k_scr.shape
    O = wo.shape[2]
    QB = 2
    G = QB * P
    GROUPS = N // G
    PAIRS = H // 2
    ROUNDS = PAIRS * GROUPS
    S_W = 2 * BANK
    S_ROW = N // S_W
    S_UNIT = QB * S_ROW
    STEPS = N // (2 * P)
    RS = 2 * STEPS
    LAG = STEPS + 3
    TRING = 4
    DIAG = 5
    TILES = 2 * S_UNIT
    WO_AT = LAG + 2 + STEPS - RS
    DRAIN = WO_AT + STEPS + 2

    with ExitStack() as ctx:
        def sb(name, shape, dt=F32):
            return ctx.enter_context(nc.sbuf_tensor(name, shape, dt))

        def sem(name):
            return ctx.enter_context(nc.semaphore(name))

        ident = sb("ident", [P, P])
        k_sb = [sb(f"k_sb{h}", [P, N], F32R) for h in range(2)]
        v_sb = [sb(f"v_sb{h}", [P, N // P, DK]) for h in range(2)]
        q_hl = [sb(f"q_hl{h}", [P, G], F32R) for h in range(2)]
        q_lh = [sb(f"q_lh{h}", [P, G], F32R) for h in range(2)]
        off_diag = sb("off_diag", [P, P])
        own = sb("own", [P, P])
        kept = sb("kept", [P, P])
        stage = [sb(f"stage{b}", [P, N]) for b in range(QB)]
        mask = [sb(f"mask{b}", [P, N], BF16) for b in range(QB)]
        row = [[sb(f"row{h}{b}", [P, N]) for b in range(QB)] for h in range(2)]
        turned = [sb(f"turned{s}", [P, 2, G]) for s in range(TRING)]
        wo_sb = sb("wo_sb", [P, H, O])
        ext = sb("ext", [P, 2, QB, S_ROW])
        nmax = sb("nmax", [P, 2, QB])
        sums = sb("sums", [P, 2, QB, S_ROW])
        rsum = sb("rsum", [P, 2, QB])
        rinv = sb("rinv", [P, 2, QB])
        o_sb = [sb(f"o_sb{h}", [P, G]) for h in range(2)]
        y_a = sb("y_a", [P, QB, O])
        y_ab = sb("y_ab", [P, QB, O])
        ps_s = [ctx.enter_context(nc.psum_tensor(f"ps_s{s}", [P, S_W], F32)) for s in range(2)]
        ps_t = [ctx.enter_context(nc.psum_tensor(f"ps_t{s}", [P, 2, G], F32)) for s in range(2)]
        ps_o = ctx.enter_context(nc.psum_tensor("ps_o", [P, BANK], F32))
        ps_y = ctx.enter_context(nc.psum_tensor("ps_y", [P, QB, O], F32))

        dve_held = sem("dve_held")
        pool_held = sem("pool_held")
        ident_zero = sem("ident_zero")
        ident_done = sem("ident_done")
        wo_in = sem("wo_in")
        k_in = [sem(f"k_in{h}") for h in range(2)]
        v_in = [sem(f"v_in{h}") for h in range(2)]
        q_in = [sem(f"q_in{h}") for h in range(2)]
        adj_in = [sem(f"adj_in{b}") for b in range(QB)]
        diag_done = sem("diag_done")
        mask_ready = sem("mask_ready")
        scored = sem("scored")
        masked = sem("masked")
        nmax_ready = sem("nmax_ready")
        exp_done = sem("exp_done")
        t_made = sem("t_made")
        t_act = sem("t_act")
        t_dve = sem("t_dve")
        pv_done = sem("pv_done")
        o_copied = sem("o_copied")
        y_made = sem("y_made")
        sum_done = sem("sum_done")
        inv_done = sem("inv_done")
        y_ready = sem("y_ready")
        y_stored = sem("y_stored")

        block = ctx.enter_context(nc.Block())

        adj_rows = adj.rearrange("(g b p) n -> g b p n", b=QB, p=P)

        @block.sync
        def _(sp):
            def load_adj(g, b):
                sp.dma_start(stage[b][:], adj_rows[g, b]).then_inc(adj_in[b], 16)

            def load_q(p, g, h):
                src = q_scr[2 * p + h, :, :, bass.ts(g, G)]
                sp.dma_start(q_hl[h][:].bitcast(F32), src.rearrange("s k n -> (s k) n")).then_inc(q_in[h], 16)
                for s in range(2):
                    sp.dma_start(q_lh[h][s * DK:(s + 1) * DK, :].bitcast(F32), src[1 - s]).then_inc(q_in[h], 16)

            def load_k(p, h):
                sp.dma_start(k_sb[h][:].bitcast(F32), k_scr[2 * p + h].rearrange("s k n -> (s k) n")).then_inc(k_in[h], 16)

            def load_v(p, h):
                sp.dma_start(v_sb[h][:], v_scr[2 * p + h]).then_inc(v_in[h], 16)

            def ahead(i, p, g, new_v=False, new_k=False):
                for b in range(QB):
                    sp.wait_ge(mask_ready, QB * i + b + 1)
                    load_adj(g, b)
                for h in range(2):
                    if new_v:
                        sp.wait_ge(pv_done, RS * i - (1 - h) * STEPS)
                        load_v(p, h)
                    sp.wait_ge(scored, TILES * i + (h + 1) * S_UNIT)
                    load_q(p, g, h)
                    if new_k:
                        load_k(p, h)

            load_q(0, 0, 0)
            load_k(0, 0)
            for b in range(QB):
                load_adj(0, b)
            load_q(0, 0, 1)
            load_k(0, 1)
            for h in range(2):
                load_v(0, h)
            for h in range(2):
                sp.dma_start(wo_sb[h * DK:(h + 1) * DK], wo.rearrange("h k o -> k h o")).then_inc(wo_in, 16)

            with sp.Fori(0, GROUPS - 1) as g:
                ahead(g, 0, g + 1)
            with sp.Fori(1, PAIRS) as p:
                ahead(p * GROUPS - 1, p, 0, new_k=True)
                ahead(p * GROUPS, p, 1, new_v=True)
                with sp.Fori(1, GROUPS - 1) as g:
                    ahead(p * GROUPS + g, p, g + 1)

        @block.gpsimd
        def _(pool):
            nc.gpsimd.memset(ident[:], 0.0).then_inc(ident_zero, 1)
            pool.wait_ge(ident_zero, 1)
            nc.gpsimd.affine_select(out=ident[:], in_=ident[:], compare_op=ALU.not_equal, fill=1.0,
                                    base=0, pattern=[[-1, P]], channel_multiplier=1).then_inc(ident_done, 1)
            pool.wait_ge(ident_done, 1)
            nc.gpsimd.tensor_scalar(off_diag[:], ident[:], -1.0, 1.0, ALU.mult, ALU.add).then_inc(ident_done, 1)
            pool.wait_ge(ident_done, 2)

            def make_mask(n, g, b):
                pool.wait_ge(adj_in[b], 16 * n + 16)
                diag = stage[b][:, bass.ds(g * G + b * P, P)]
                done = DIAG * (QB * n + b)
                nc.gpsimd.tensor_copy(own[:], diag).then_inc(diag_done, 1)
                nc.gpsimd.tensor_tensor(kept[:], diag, off_diag[:], ALU.mult).then_inc(diag_done, 1)
                pool.wait_ge(diag_done, done + 2)
                pool.sem_inc(pool_held, 1)
                nc.gpsimd.tensor_scalar(own[:], own[:], 1.0, None, ALU.max).then_inc(diag_done, 1)
                pool.wait_ge(diag_done, done + 3)
                nc.gpsimd.tensor_tensor(own[:], own[:], ident[:], ALU.mult).then_inc(diag_done, 1)
                pool.wait_ge(diag_done, done + 4)
                pool.sem_inc(pool_held, 1)
                nc.gpsimd.tensor_tensor(diag, kept[:], own[:], ALU.add).then_inc(diag_done, 1)
                pool.wait_ge(diag_done, done + DIAG)
                read = S_UNIT * (2 * n - 1) + (b + 1) * S_ROW
                if due(read) and due(n):
                    pool.wait_ge(masked, read)
                pool.sem_inc(pool_held, 1)
                nc.gpsimd.tensor_scalar(mask[b][:], stage[b][:], -1.0, -BIG, ALU.add, ALU.mult)\
                    .then_inc(mask_ready, 1)

            def store_y(n):
                pool.wait_ge(y_ready, QB * n + QB)
                pool.dma_start(y_scr[n].rearrange("b p o -> p b o"), y_ab[:]).then_inc(y_stored, 16)

            for b in range(QB):
                make_mask(0, 0, b)
            for b in range(QB):
                make_mask(1, 1, b)
            with pool.Fori(2, ROUNDS) as n:
                store_y(n - 2)
                g = n % GROUPS
                for b in range(QB):
                    make_mask(n, g, b)
            store_y(ROUNDS - 2)
            store_y(ROUNDS - 1)
            pool.wait_ge(y_stored, 16 * ROUNDS)

        @block.tensor
        def _(pe):
            pe.wait_ge(ident_done, 1)

            def scores(i, s):
                h, j = s // STEPS, s % STEPS
                b, c = j // (STEPS // QB), j % (STEPS // QB)
                m = s // 2
                if j == 0:
                    pe.wait_ge(q_in[h], 48 * i + 48)
                    pe.wait_ge(k_in[h], 16 * (i // GROUPS) + 16)
                if s % 2 == 0 and due(TILES * i + m - 1):
                    pe.wait_ge(masked, TILES * i + (m - 1))
                out = ps_s[m % 2][:, (s % 2) * BANK:(s % 2 + 1) * BANK]
                keys = k_sb[h][:, c * BANK:(c + 1) * BANK]
                nc.tensor.matmul(out, q_hl[h][:, b * P:(b + 1) * P], keys, start=True, stop=False)
                last = nc.tensor.matmul(out, q_lh[h][:, b * P:(b + 1) * P], keys, start=False, stop=True)
                if s % 2 == 1:
                    last.then_inc(scored, 1)

            def turn(i, t):
                h, j = t // STEPS, t % STEPS
                c = j // (STEPS // S_ROW)
                if j % (STEPS // S_ROW) == 0:
                    pe.wait_ge(exp_done, TILES * i + (h * S_UNIT + S_ROW + c + 1))
                if due(STEPS * i + t // 2):
                    pe.wait_ge((t_act, t_dve)[t % 2], STEPS * i + t // 2)
                for k in range(2):
                    for b in range(QB):
                        last = nc.tensor.transpose(ps_t[t % 2][:, k, b * P:(b + 1) * P],
                                                   row[h][b][:, (2 * j + k) * P:(2 * j + k + 1) * P], ident[:])
                last.then_inc(t_made, 1)

            def times_v(i, t):
                h, j = t // STEPS, t % STEPS
                if j == 0:
                    pe.wait_ge(v_in[h], 16 * (i // GROUPS) + 16)
                    if due(2 * i + h):
                        pe.wait_ge(o_copied, 2 * i + h)
                pe.wait_ge((t_act, t_dve)[t % 2], STEPS * i + (t // 2 + 1))
                for k in range(2):
                    last = nc.tensor.matmul(ps_o[k * DK:(k + 1) * DK, 0:G], v_sb[h][:, 2 * j + k, :],
                                            turned[t % TRING][:, k, :], start=(j == 0), stop=(j == STEPS - 1))
                last.then_inc(pv_done, 1)

            def times_wo(i, h):
                pe.wait_ge(o_copied, 2 * i + h + 1)
                for b in range(QB):
                    last = nc.tensor.matmul(ps_y[:, b, :], o_sb[h][:, b * P:(b + 1) * P],
                                            wo_sb[:, bass.ds(2 * (i // GROUPS) + h, 1), :].rearrange("p a o -> p (a o)"),
                                            start=True, stop=True)
                last.then_inc(y_made, 1)

            def steps(i, n, scoring=True):
                for s in range(n):
                    if scoring:
                        scores(i, s)
                    for part, lag in ((turn, LAG), (times_v, LAG + 1)):
                        if s >= lag and scoring:
                            part(i, s - lag)
                        elif s < lag and due(i):
                            part(i - 1, s - lag + RS)
                    for h in range(2):
                        if s == WO_AT + h * STEPS and due(i):
                            times_wo(i - 1, h)

            pe.wait_ge(wo_in, 32)
            steps(0, RS)
            steps(1, RS)
            with pe.Fori(2, ROUNDS) as i:
                steps(i, RS)
            steps(ROUNDS, DRAIN, scoring=False)

        @block.scalar
        def _(act):
            def exp_tile(i, h, b, c):
                if c == 0:
                    act.wait_ge(nmax_ready, 2 * QB * i + (h * QB + b + 1))
                tile = row[h][b][:, c * S_W:(c + 1) * S_W]
                nc.scalar.activation(tile, tile, ACT.Exp, bias=nmax[:, h, b:b + 1], scale=-1.0,
                                     accum_out=sums[:, h, b, c:c + 1]).then_inc(exp_done, 1)

            def copy_turned(i, t):
                act.wait_ge(t_made, RS * i + t + 1)
                if due(RS * i + t + 1 - TRING):
                    act.wait_ge(pv_done, RS * i + (t + 1 - TRING))
                nc.scalar.copy(turned[t % TRING][:], ps_t[0][:]).then_inc(t_act, 1)

            def steps(i, n, scoring=True):
                for s in range(n):
                    if (s - LAG) % 2 == 0:
                        if s >= LAG and scoring:
                            copy_turned(i, s - LAG)
                        elif s < LAG and due(i):
                            copy_turned(i - 1, s - LAG + RS)
                    for u in range(2 * QB):
                        for c in range(S_ROW):
                            at = (u + 1) * (STEPS // QB) + 2 * c
                            if at == s and scoring:
                                exp_tile(i, u // QB, u % QB, c)
                            elif at == s + RS and due(i):
                                exp_tile(i - 1, u // QB, u % QB, c)

            steps(0, RS)
            steps(1, RS)
            with act.Fori(2, ROUNDS) as i:
                steps(i, RS)
            steps(ROUNDS, LAG, scoring=False)

        @block.vector
        def _(dve):
            def mask_tile(i, m):
                h, b, c = m // S_UNIT, m // S_ROW % QB, m % S_ROW
                if c == 0 and h == 0:
                    dve.wait_ge(mask_ready, QB * i + (b + 1))
                if due(i):
                    dve.wait_ge(t_made, RS * i + (h * STEPS + (c + 1) * (STEPS // S_ROW) - RS))
                dve.wait_ge(scored, TILES * i + (m + 1))
                dve.sem_inc(dve_held, 1)
                nc.vector.tensor_tensor_reduce(row[h][b][:, c * S_W:(c + 1) * S_W], ps_s[m % 2][:],
                                               mask[b][:, c * S_W:(c + 1) * S_W], 1.0, 3e38,
                                               ALU.add, ALU.min, ext[:, h, b, c:c + 1]).then_inc(masked, 1)
                if c == S_ROW - 1:
                    dve.wait_ge(masked, TILES * i + (m + 1))
                    nc.vector.tensor_reduce(nmax[:, h, b:b + 1], ext[:, h, b, :], AX.X, ALU.min)\
                        .then_inc(nmax_ready, 1)

            def copy_turned(i, t):
                dve.wait_ge(t_made, RS * i + (t + 1))
                if due(RS * i + t + 1 - TRING):
                    dve.wait_ge(pv_done, RS * i + (t + 1 - TRING))
                nc.vector.tensor_copy(turned[t % TRING][:], ps_t[1][:]).then_inc(t_dve, 1)

            def copy_o(i, h):
                dve.wait_ge(pv_done, RS * i + (h + 1) * STEPS)
                nc.vector.tensor_copy(o_sb[h][:], ps_o[:, 0:G]).then_inc(o_copied, 1)
                nc.vector.tensor_reduce(rsum[:, h, :], sums[:, h, :, :], AX.X, ALU.add).then_inc(sum_done, 1)
                dve.wait_ge(sum_done, 2 * i + (h + 1))
                nc.vector.reciprocal(rinv[:, h, :], rsum[:, h, :]).then_inc(inv_done, 1)

            def scale_y(i, h):
                dve.wait_ge(inv_done, 2 * i + (h + 1))
                if h == 1 and due(i):
                    dve.wait_ge(y_stored, 16 * i)
                dve.wait_ge(y_made, 2 * i + (h + 1))
                for b in range(QB):
                    if h == 0:
                        nc.vector.tensor_scalar(y_a[:, b, :], ps_y[:, b, :], rinv[:, 0, b:b + 1], None, ALU.mult)
                    else:
                        nc.vector.scalar_tensor_tensor(out=y_ab[:, b, :], in0=ps_y[:, b, :],
                                                       scalar=rinv[:, 1, b:b + 1], in1=y_a[:, b, :],
                                                       op0=ALU.mult, op1=ALU.add).then_inc(y_ready, 1)

            def steps(i, n, scoring=True):
                for s in range(n):
                    if (s - LAG) % 2 == 1:
                        if s >= LAG and scoring:
                            copy_turned(i, s - LAG)
                        elif s < LAG and due(i):
                            copy_turned(i - 1, s - LAG + RS)
                    if scoring and s % 2 == 1:
                        mask_tile(i, s // 2)
                    for h in range(2):
                        if s == WO_AT - 1 + h * STEPS and due(i):
                            copy_o(i - 1, h)
                        if s == WO_AT + 1 + h * STEPS and due(i):
                            scale_y(i - 1, h)

            steps(0, RS)
            steps(1, RS)
            with dve.Fori(2, ROUNDS) as i:
                steps(i, RS)
            steps(ROUNDS, DRAIN, scoring=False)


def residual_norm(nc, x, y_scr, out):
    N, D = x.shape
    ROUNDS, QB = y_scr.shape[:2]
    GROUPS = N // (QB * P)
    PAIRS = ROUNDS // GROUPS
    W = 2
    TB = W * QB
    TILES = GROUPS // W
    with ExitStack() as ctx:
        def sb(name, shape, dt=F32):
            return ctx.enter_context(nc.sbuf_tensor(name, shape, dt))

        def sem(name):
            return ctx.enter_context(nc.semaphore(name))

        part = [[sb(f"part{u}{k}", [P, TB, D]) for k in range(PAIRS + 1)] for u in range(2)]
        stats = [sb(f"stats{u}", [P, TB, 6]) for u in range(2)]
        mv = [sb(f"mv{u}", [P, TB, 2]) for u in range(2)]
        var = [sb(f"var{u}", [P, TB]) for u in range(2)]
        std = [sb(f"std{u}", [P, TB]) for u in range(2)]
        rstd = [sb(f"rstd{u}", [P, TB]) for u in range(2)]
        normed = [sb(f"normed{u}", [P, TB, D]) for u in range(2)]
        part_in = [[sem(f"part_in{u}{k}") for k in range(PAIRS + 1)] for u in range(2)]
        dve_held = sem("norm_held")
        link = sem("link")
        var_ready = sem("var_ready")
        std_ready = sem("std_ready")
        normed_ready = sem("normed_ready")
        stored = [sem(f"out_stored{u}") for u in range(2)]
        LINKS = PAIRS + 3
        block = ctx.enter_context(nc.Block())

        @block.sync
        def _(sp):
            x_tiles = x.rearrange("(t b p) d -> t p b d", p=P, b=TB)
            y_tiles = y_scr.rearrange("(k t w) b p o -> k t p (w b) o", k=PAIRS, w=W)

            def load(t, u):
                sp.dma_start(part[u][PAIRS][:], x_tiles[t]).then_inc(part_in[u][PAIRS], 16)
                for k in range(PAIRS):
                    sp.dma_start(part[u][k][:], y_tiles[k, t]).then_inc(part_in[u][k], 16)

            for u in range(2):
                load(u, u)
            with sp.Fori(1, TILES // 2) as r:
                for u in range(2):
                    sp.wait_ge(normed_ready, 2 * r + (u - 1))
                    load(2 * r + u, u)

        @block.vector
        def _(dve):
            def tile_(r, u):
                t = 2 * r + u

                def chained(ins, k):
                    ins.then_inc(link, 1)
                    dve.wait_ge(link, LINKS * t + k + 1)

                total = part[u][PAIRS]
                dve.wait_ge(part_in[u][PAIRS], 16 * r + 16)
                for k in range(PAIRS):
                    dve.wait_ge(part_in[u][k], 16 * r + 16)
                    chained(nc.vector.tensor_tensor(total[:], total[:], part[u][k][:], ALU.add), k)
                for b in range(TB):
                    last = nc.vector.bn_stats(stats[u][:, b, :], total[:, b, :])
                last.then_inc(link, 1)
                dve.wait_ge(link, LINKS * t + PAIRS + 1)
                dve.sem_inc(dve_held, 1)
                for b in range(TB):
                    last = nc.vector.bn_aggr(mv[u][:, b, :], stats[u][:, b, :])
                chained(last, PAIRS + 1)
                nc.vector.tensor_scalar(var[u][:], mv[u][:, :, 1], EPS, None, ALU.add).then_inc(var_ready, 1)
                dve.wait_ge(std_ready, t + 1)
                chained(nc.vector.reciprocal(rstd[u][:], std[u][:]), PAIRS + 2)
                if due(r):
                    dve.wait_ge(stored[u], 16 * r)
                for b in range(TB):
                    last = nc.vector.tensor_scalar(normed[u][:, b, :], total[:, b, :], mv[u][:, b, 0:1],
                                                   rstd[u][:, b:b + 1], ALU.subtract, ALU.mult)
                last.then_inc(normed_ready, 1)

            tile_(0, 0)
            tile_(0, 1)
            with dve.Fori(1, TILES // 2) as r:
                tile_(r, 0)
                tile_(r, 1)

        @block.scalar
        def _(act):
            out_tiles = out.rearrange("(t b p) d -> t p b d", p=P, b=TB)

            def tile_(r, u):
                t = 2 * r + u
                act.wait_ge(var_ready, t + 1)
                nc.scalar.activation(std[u][:], var[u][:], ACT.Sqrt).then_inc(std_ready, 1)
                act.wait_ge(normed_ready, t + 1)
                act.dma_start(out_tiles[t], normed[u][:]).then_inc(stored[u], 16)

            tile_(0, 0)
            tile_(0, 1)
            with act.Fori(1, TILES // 2) as r:
                tile_(r, 0)
                tile_(r, 1)
            for u in range(2):
                act.wait_ge(stored[u], 16 * (TILES // 2))


def graph_attention(nc, x, adj, wk, wq, wv, wo, out):
    N, D = x.shape
    H, _, DK = wk.shape
    O = wo.shape[2]
    q_scr = nc.dram_tensor("q_scr", [H, 2, DK, N], F32).ap()
    k_scr = nc.dram_tensor("k_scr", [H, 2, DK, N], F32).ap()
    v_scr = nc.dram_tensor("v_scr", [H, P, N // P, DK], F32).ap()
    y_scr = nc.dram_tensor("y_scr", [(H // 2) * (N // (2 * P)), 2, P, O], F32).ap()
    projections(nc, x, wk, wq, wv, q_scr, k_scr, v_scr)
    attention(nc, adj, wo, q_scr, k_scr, v_scr, y_scr)
    residual_norm(nc, x, y_scr, out)


_INS = ['x', 'adj', 'L0_gnn_Wks', 'L0_gnn_Wqs', 'L0_gnn_Wvs', 'L0_gnn_Wo']
_OUTS = [((4096, 256), 'float32')]


def kernel(**inputs):
    import numpy as _np
    import concourse.bacc as _bacc
    from concourse import mybir as _mybir
    from concourse.bass_utils import run_bass_kernel_spmd as _run

    nc = _bacc.Bacc("TRN2", target_bir_lowering=False, num_devices=1)
    arrays, args = {}, []
    for name in _INS:
        a = _np.ascontiguousarray(inputs[name])
        arrays[f"in_{name}_dram"] = a
        args.append(nc.dram_tensor(f"in_{name}_dram", a.shape, _mybir.dt.from_np(a.dtype), kind="ExternalInput").ap())
    for i, (shape, dtype) in enumerate(_OUTS):
        dt = _mybir.dt.from_np(_np.dtype(dtype))
        args.append(nc.dram_tensor(f"out_{i}_dram", shape, dt, kind="ExternalOutput").ap())
    graph_attention(nc, *args)
    r = _run(nc, [arrays], core_ids=[0])
    return r.results[0]["out_0_dram"]
```

```python
from contextlib import ExitStack

import concourse.bass as bass
from concourse import mybir

ALU = mybir.AluOpType
ACT = mybir.ActivationFunctionType
AX = mybir.AxisListType
F32 = mybir.dt.float32
F32R = mybir.dt.float32r
BF16 = mybir.dt.bfloat16

P = 128
BANK = 512
BIG = 1e16
EPS = 1e-5


def due(n):
    return not isinstance(n, int) or n > 0


def projections(nc, x, wk, wq, wv, q_scr, k_scr, v_scr, vb_scr):
    N, D = x.shape
    H, _, DK = wk.shape
    CD = D // P
    CB = BANK // P
    CHUNKS = N // BANK
    PAIRS = H // 2
    TILES = 2 * PAIRS
    RING = 4
    with ExitStack() as ctx:
        def sb(name, shape, dt=F32):
            return ctx.enter_context(nc.sbuf_tensor(name, shape, dt))

        def sem(name):
            return ctx.enter_context(nc.semaphore(name))

        ident = sb("p_ident", [P, P])
        w_sb = [sb("wk_sb", [P, CD, H * DK]), sb("wq_sb", [P, CD, H * DK])]
        wv_sb = sb("wv_sb", [P, CD, H * DK])
        xin = [sb(f"xin{u}", [P, CB, D]) for u in range(2)]
        xT = [sb(f"xT{u}", [P, CD, BANK]) for u in range(2)]
        high = [sb(f"high{s}", [P, BANK], F32R) for s in range(RING)]
        low = [sb(f"low{s}", [P, BANK], F32R) for s in range(RING)]
        v_hl = [sb(f"v_hl{u}", [P, H, CB, 2, DK], F32R) for u in range(2)]
        v_bf = [sb(f"v_bf{u}", [P, H, CB, DK], BF16) for u in range(2)]
        ps_x = [ctx.enter_context(nc.psum_tensor(f"ps_x{c}", [P, BANK], F32)) for c in range(CD)]
        ps_p = [ctx.enter_context(nc.psum_tensor(f"ps_p{s}", [P, BANK], F32)) for s in range(4)]
        ps_v = [ctx.enter_context(nc.psum_tensor(f"ps_v{s}", [P, BANK], F32)) for s in range(2)]

        weights_in = sem("weights_in")
        x_in = [sem(f"x_in{u}") for u in range(2)]
        ident_zero = sem("p_ident_zero")
        ident_done = sem("p_ident_done")
        x_turned = sem("x_turned")
        xT_act = sem("xT_act")
        xT_dve = sem("xT_dve")
        projected = sem("projected")
        high_done = sem("high_done")
        low_done = sem("low_done")
        stored = [sem(f"stored{s}") for s in range(RING)]
        v_made = sem("v_made")
        v_high = sem("v_high")
        v_low = sem("v_low")
        v_stored = [sem(f"v_stored{u}") for u in range(2)]

        block = ctx.enter_context(nc.Block())

        @block.gpsimd
        def _(pool):
            nc.gpsimd.memset(ident[:], 0.0).then_inc(ident_zero, 1)
            pool.wait_ge(ident_zero, 1)
            nc.gpsimd.affine_select(out=ident[:], in_=ident[:], compare_op=ALU.not_equal, fill=1.0,
                                    base=0, pattern=[[-1, P]], channel_multiplier=1).then_inc(ident_done, 1)
            xd = x.rearrange("(n b p) d -> n p b d", p=P, b=CB)
            for u in range(2):
                pool.dma_start(xin[u][:], xd[u]).then_inc(x_in[u], 16)
            with pool.Fori(1, CHUNKS // 2) as r:
                for u in range(2):
                    pool.wait_ge(x_turned, 2 * r + (u - 1))
                    pool.dma_start(xin[u][:], xd[2 * r + u]).then_inc(x_in[u], 16)

        @block.sync
        def _(sp):
            for w, t in ((wk, w_sb[0]), (wq, w_sb[1]), (wv, wv_sb)):
                for c in range(CD):
                    sp.dma_start(t[:, c, :].rearrange("p (h k) -> p h k", h=H),
                                 w[:, c * P:(c + 1) * P, :].rearrange("h p k -> p h k")).then_inc(weights_in, 16)
            def chunk(r, u):
                n = 2 * r + u
                for t in range(TILES):
                    s, pair, scr = t % RING, t // 2, (k_scr, q_scr)[t % 2]
                    sp.wait_ge(high_done, n * TILES + (t + 1))
                    for hh in range(2):
                        sp.dma_start(scr[2 * pair + hh, 0, :, bass.ts(n, BANK)],
                                     high[s][hh * DK:(hh + 1) * DK, :].bitcast(F32)).then_inc(stored[s], 16)
                    sp.wait_ge(low_done, n * TILES + (t + 1))
                    for hh in range(2):
                        sp.dma_start(scr[2 * pair + hh, 1, :, bass.ts(n, BANK)],
                                     low[s][hh * DK:(hh + 1) * DK, :].bitcast(F32)).then_inc(stored[s], 16)
                sp.wait_ge(v_high, n * CB + CB)
                sp.wait_ge(v_low, n * CB + CB)
                sp.dma_start(v_scr[:, :, bass.ts(n, CB), :].rearrange("h p b k -> p h b k"),
                             v_hl[u][:].rearrange("p h b s k -> p h b (s k)").bitcast(F32)).then_inc(v_stored[u], 16)
                sp.dma_start(vb_scr[:, :, bass.ts(n, CB), :].rearrange("h p b k -> p h b k"),
                             v_bf[u][:]).then_inc(v_stored[u], 16)

            with sp.Fori(0, CHUNKS // 2) as r:
                chunk(r, 0)
                chunk(r, 1)
            for u in range(2):
                sp.wait_ge(v_stored[u], 32 * (CHUNKS // 2))
            for s in range(RING):
                sp.wait_ge(stored[s], 64 * CHUNKS * TILES // RING)

        @block.tensor
        def _(pe):
            pe.wait_ge(ident_done, 1)

            def chunk(r, u, first):
                n = 2 * r + u
                pe.wait_ge(x_in[u], 16 * r + 16)
                if not first:
                    pe.wait_ge(xT_act, n)
                    pe.wait_ge(xT_dve, n)
                for c in range(CD):
                    for b in range(CB):
                        last = nc.tensor.transpose(ps_x[c][:, b * P:(b + 1) * P],
                                                   xin[u][:, b, c * P:(c + 1) * P], ident[:])
                last.then_inc(x_turned, 1)
                if first:
                    pe.wait_ge(weights_in, 16 * 3 * CD)
                pe.wait_ge(xT_act, n + 1)
                pe.wait_ge(xT_dve, n + 1)
                for t in range(TILES):
                    w = w_sb[t % 2]
                    pair = t // 2
                    if not first or t >= 4:
                        pe.wait_ge(low_done, n * TILES + (t - 3))
                    for c in range(CD):
                        last = nc.tensor.matmul(ps_p[t % 4][:], w[:, c, pair * P:(pair + 1) * P],
                                                xT[u][:, c, :], start=(c == 0), stop=(c == CD - 1))
                    last.then_inc(projected, 1)
                for b in range(CB):
                    if not first or b >= 2:
                        pe.wait_ge(v_high, n * CB + (b - 1))
                        pe.wait_ge(v_low, n * CB + (b - 1))
                    for c in range(CD):
                        last = nc.tensor.matmul(ps_v[b % 2][:], xT[u][:, c, b * P:(b + 1) * P],
                                                wv_sb[:, c, :], start=(c == 0), stop=(c == CD - 1))
                    last.then_inc(v_made, 1)

            chunk(0, 0, True)
            chunk(0, 1, False)
            with pe.Fori(1, CHUNKS // 2) as r:
                chunk(r, 0, False)
                chunk(r, 1, False)

        def heads(bank):
            return bank[:].rearrange("p (h k) -> p h k", h=H)

        @block.scalar
        def _(act):
            def chunk(r, u, first):
                n = 2 * r + u
                act.wait_ge(x_turned, n + 1)
                if not first:
                    act.wait_ge(v_made, (n - 1) * CB)
                nc.scalar.copy(xT[u][:, 0, :], ps_x[0][:]).then_inc(xT_act, 1)
                for t in range(TILES):
                    act.wait_ge(projected, n * TILES + (t + 1))
                    if not first or t >= RING:
                        act.wait_ge(stored[t % RING], 64 * ((TILES // RING) * n + t // RING))
                    nc.scalar.activation(high[t % RING][:], ps_p[t % 4][:], ACT.Copy,
                                         scale=(1.0, -(DK ** -0.5))[t % 2]).then_inc(high_done, 1)
                if due(r):
                    act.wait_ge(v_stored[u], 32 * r)
                for b in range(CB):
                    act.wait_ge(v_made, n * CB + (b + 1))
                    nc.scalar.copy(v_hl[u][:, :, b, 0, :], heads(ps_v[b % 2]))
                    nc.scalar.copy(v_bf[u][:, :, b, :], heads(ps_v[b % 2])).then_inc(v_high, 1)

            chunk(0, 0, True)
            chunk(0, 1, False)
            with act.Fori(1, CHUNKS // 2) as r:
                chunk(r, 0, False)
                chunk(r, 1, False)

        @block.vector
        def _(dve):
            def chunk(r, u, first):
                n = 2 * r + u
                dve.wait_ge(x_turned, n + 1)
                if not first:
                    dve.wait_ge(v_made, (n - 1) * CB)
                nc.vector.tensor_copy(xT[u][:, 1, :], ps_x[1][:]).then_inc(xT_dve, 1)
                for t in range(TILES):
                    dve.wait_ge(high_done, n * TILES + (t + 1))
                    if not first or t >= RING:
                        dve.wait_ge(stored[t % RING], 64 * ((TILES // RING) * n + t // RING))
                    nc.vector.scalar_tensor_tensor(out=low[t % RING][:], in0=ps_p[t % 4][:],
                                                   scalar=(1.0, -(DK ** -0.5))[t % 2],
                                                   in1=high[t % RING][:].bitcast(F32),
                                                   op0=ALU.mult, op1=ALU.subtract).then_inc(low_done, 1)
                for b in range(CB):
                    dve.wait_ge(v_high, n * CB + (b + 1))
                    nc.vector.tensor_tensor(v_hl[u][:, :, b, 1, :], heads(ps_v[b % 2]),
                                            v_hl[u][:, :, b, 0, :].bitcast(F32), ALU.subtract).then_inc(v_low, 1)

            chunk(0, 0, True)
            chunk(0, 1, False)
            with dve.Fori(1, CHUNKS // 2) as r:
                chunk(r, 0, False)
                chunk(r, 1, False)


def attention(nc, adj, wo, q_scr, k_scr, v_scr, vb_scr, y_scr):
    H, _, DK, N = k_scr.shape
    O = wo.shape[2]
    QB = 2
    G = QB * P
    GROUPS = N // G
    PAIRS = H // 2
    ROUNDS = PAIRS * GROUPS
    S_W = BANK
    S_RING = 2
    T_RING = 4
    S_ROW = N // S_W
    S_UNIT = QB * S_ROW
    E_W = 2 * S_W
    E_ROW = N // E_W
    E_UNIT = QB * E_ROW
    STEPS = N // (2 * P)
    RS = 2 * STEPS
    LAG = STEPS + 3
    PV_LAG = LAG + 3
    TRING = 4
    DIAG = 5
    TILES = 2 * S_UNIT
    EXPS = 2 * E_UNIT
    OUT_AT = PV_LAG + STEPS - RS
    DRAIN = OUT_AT + STEPS + 4

    with ExitStack() as ctx:
        def sb(name, shape, dt=F32):
            return ctx.enter_context(nc.sbuf_tensor(name, shape, dt))

        def sem(name):
            return ctx.enter_context(nc.semaphore(name))

        ident = sb("ident", [P, P])
        k_sb = [sb(f"k_sb{h}", [P, N], F32R) for h in range(2)]
        v_sb = [sb(f"v_sb{h}", [P, N // P, 2 * DK], F32R) for h in range(2)]
        vb_sb = [sb(f"vb_sb{h}", [P, N // P, DK], BF16) for h in range(2)]
        q_hl = [sb(f"q_hl{h}", [P, G], F32R) for h in range(2)]
        q_lh = [sb(f"q_lh{h}", [P, G], F32R) for h in range(2)]
        off_diag = sb("off_diag", [P, P])
        own = sb("own", [P, P])
        kept = sb("kept", [P, P])
        stage = [sb(f"stage{b}", [P, N]) for b in range(QB)]
        mask = [sb(f"mask{b}", [P, N], BF16) for b in range(QB)]
        row = [[sb(f"row{h}{b}", [P, N]) for b in range(QB)] for h in range(2)]
        high = [sb(f"high_w{s}", [P, 2, G], F32R) for s in range(TRING)]
        low = [sb(f"low_w{s}", [P, 2, G], BF16) for s in range(TRING)]
        wo_sb = sb("wo_sb", [P, H, O])
        ext = sb("ext", [P, 2, QB, S_ROW])
        nmax = sb("nmax", [P, 2, QB])
        sums = sb("sums", [P, 2, QB, E_ROW])
        rsum = sb("rsum", [P, 2, QB])
        rinv = sb("rinv", [P, 2, QB])
        o_sb = [sb(f"o_sb{h}", [P, G]) for h in range(2)]
        y_a = sb("y_a", [P, QB, O])
        y_ab = sb("y_ab", [P, QB, O])
        ps_s = [ctx.enter_context(nc.psum_tensor(f"ps_s{s}", [P, S_W], F32)) for s in range(S_RING)]
        ps_t = [ctx.enter_context(nc.psum_tensor(f"ps_t{s}", [P, 2, G], F32)) for s in range(T_RING)]
        ps_oy = [ctx.enter_context(nc.psum_tensor(f"ps_oy{h}", [P, QB, O], F32)) for h in range(2)]

        dve_held = sem("dve_held")
        pool_held = sem("pool_held")
        ident_zero = sem("ident_zero")
        ident_done = sem("ident_done")
        wo_in = sem("wo_in")
        k_in = [sem(f"k_in{h}") for h in range(2)]
        v_in = [sem(f"v_in{h}") for h in range(2)]
        q_in = [sem(f"q_in{h}") for h in range(2)]
        adj_in = [sem(f"adj_in{b}") for b in range(QB)]
        diag_done = sem("diag_done")
        mask_ready = sem("mask_ready")
        scored = sem("scored")
        masked = sem("masked")
        nmax_ready = sem("nmax_ready")
        exp_done = sem("exp_done")
        t_made = sem("t_made")
        high_done = sem("high_w_done")
        low_done = sem("low_w_done")
        pv_done = sem("pv_done")
        o_copied = sem("o_copied")
        y_made = sem("y_made")
        sum_done = sem("sum_done")
        inv_done = sem("inv_done")
        ya_done = sem("ya_done")
        y_ready = sem("y_ready")
        y_stored = sem("y_stored")

        block = ctx.enter_context(nc.Block())

        adj_rows = adj.rearrange("(g b p) n -> g b p n", b=QB, p=P)

        @block.sync
        def _(sp):
            def load_adj(g, b):
                sp.dma_start(stage[b][:], adj_rows[g, b]).then_inc(adj_in[b], 16)

            def load_q(p, g, h):
                src = q_scr[2 * p + h, :, :, bass.ts(g, G)]
                sp.dma_start(q_hl[h][:].bitcast(F32), src.rearrange("s k n -> (s k) n")).then_inc(q_in[h], 16)
                for s in range(2):
                    sp.dma_start(q_lh[h][s * DK:(s + 1) * DK, :].bitcast(F32), src[1 - s]).then_inc(q_in[h], 16)

            def load_k(p, h):
                sp.dma_start(k_sb[h][:].bitcast(F32), k_scr[2 * p + h].rearrange("s k n -> (s k) n")).then_inc(k_in[h], 16)

            def load_v(p, h):
                sp.dma_start(v_sb[h][:].bitcast(F32), v_scr[2 * p + h]).then_inc(v_in[h], 16)
                sp.dma_start(vb_sb[h][:], vb_scr[2 * p + h]).then_inc(v_in[h], 16)

            def ahead(i, p, g, new_v=False, new_k=False):
                for b in range(QB):
                    sp.wait_ge(mask_ready, QB * i + b + 1)
                    load_adj(g, b)
                for h in range(2):
                    if new_v:
                        sp.wait_ge(pv_done, RS * i - (1 - h) * STEPS)
                        load_v(p, h)
                    sp.wait_ge(scored, TILES * i + (h + 1) * S_UNIT)
                    load_q(p, g, h)
                    if new_k:
                        load_k(p, h)

            load_q(0, 0, 0)
            load_k(0, 0)
            for b in range(QB):
                load_adj(0, b)
            load_q(0, 0, 1)
            load_k(0, 1)
            for h in range(2):
                load_v(0, h)
            for h in range(2):
                sp.dma_start(wo_sb[h * DK:(h + 1) * DK], wo.rearrange("h k o -> k h o")).then_inc(wo_in, 16)

            with sp.Fori(0, GROUPS - 1) as g:
                ahead(g, 0, g + 1)
            with sp.Fori(1, PAIRS) as p:
                ahead(p * GROUPS - 1, p, 0, new_k=True)
                ahead(p * GROUPS, p, 1, new_v=True)
                with sp.Fori(1, GROUPS - 1) as g:
                    ahead(p * GROUPS + g, p, g + 1)

        @block.gpsimd
        def _(pool):
            nc.gpsimd.memset(ident[:], 0.0).then_inc(ident_zero, 1)
            pool.wait_ge(ident_zero, 1)
            nc.gpsimd.affine_select(out=ident[:], in_=ident[:], compare_op=ALU.not_equal, fill=1.0,
                                    base=0, pattern=[[-1, P]], channel_multiplier=1).then_inc(ident_done, 1)
            pool.wait_ge(ident_done, 1)
            nc.gpsimd.tensor_scalar(off_diag[:], ident[:], -1.0, 1.0, ALU.mult, ALU.add).then_inc(ident_done, 1)
            pool.wait_ge(ident_done, 2)

            def make_mask(n, g, b):
                pool.wait_ge(adj_in[b], 16 * n + 16)
                diag = stage[b][:, bass.ds(g * G + b * P, P)]
                done = DIAG * (QB * n + b)
                nc.gpsimd.tensor_copy(own[:], diag).then_inc(diag_done, 1)
                nc.gpsimd.tensor_tensor(kept[:], diag, off_diag[:], ALU.mult).then_inc(diag_done, 1)
                pool.wait_ge(diag_done, done + 2)
                pool.sem_inc(pool_held, 1)
                nc.gpsimd.tensor_scalar(own[:], own[:], 1.0, None, ALU.max).then_inc(diag_done, 1)
                pool.wait_ge(diag_done, done + 3)
                nc.gpsimd.tensor_tensor(own[:], own[:], ident[:], ALU.mult).then_inc(diag_done, 1)
                pool.wait_ge(diag_done, done + 4)
                pool.sem_inc(pool_held, 1)
                nc.gpsimd.tensor_tensor(diag, kept[:], own[:], ALU.add).then_inc(diag_done, 1)
                pool.wait_ge(diag_done, done + DIAG)
                read = S_UNIT * (2 * n - 1) + (b + 1) * S_ROW
                if due(read) and due(n):
                    pool.wait_ge(masked, read)
                pool.sem_inc(pool_held, 1)
                nc.gpsimd.tensor_scalar(mask[b][:], stage[b][:], -1.0, -BIG, ALU.add, ALU.mult)\
                    .then_inc(mask_ready, 1)

            def store_y(n):
                pool.wait_ge(y_ready, QB * n + QB)
                pool.dma_start(y_scr[n].rearrange("b p o -> p b o"), y_ab[:]).then_inc(y_stored, 16)

            for b in range(QB):
                make_mask(0, 0, b)
            for b in range(QB):
                make_mask(1, 1, b)
            with pool.Fori(2, ROUNDS) as n:
                store_y(n - 2)
                g = n % GROUPS
                for b in range(QB):
                    make_mask(n, g, b)
            store_y(ROUNDS - 2)
            store_y(ROUNDS - 1)
            pool.wait_ge(y_stored, 16 * ROUNDS)

        @block.tensor
        def _(pe):
            pe.wait_ge(ident_done, 1)

            def scores(i, s):
                h, j = s // STEPS, s % STEPS
                b, c = j // S_ROW, j % S_ROW
                if j == 0:
                    pe.wait_ge(q_in[h], 48 * i + 48)
                    pe.wait_ge(k_in[h], 16 * (i // GROUPS) + 16)
                if due(TILES * i + s + 1 - S_RING):
                    pe.wait_ge(masked, TILES * i + (s + 1 - S_RING))
                keys = k_sb[h][:, c * S_W:(c + 1) * S_W]
                nc.tensor.matmul(ps_s[s % S_RING][:], q_hl[h][:, b * P:(b + 1) * P], keys, start=True, stop=False)
                nc.tensor.matmul(ps_s[s % S_RING][:], q_lh[h][:, b * P:(b + 1) * P], keys, start=False, stop=True)\
                    .then_inc(scored, 1)

            def turn(i, t):
                h, j = t // STEPS, t % STEPS
                c = j // (STEPS // E_ROW)
                if j % (STEPS // E_ROW) == 0:
                    pe.wait_ge(exp_done, EXPS * i + (h * E_UNIT + E_ROW + c + 1))
                if due(RS * i + t + 1 - T_RING):
                    pe.wait_ge(low_done, RS * i + (t + 1 - T_RING))
                for k in range(2):
                    for b in range(QB):
                        last = nc.tensor.transpose(ps_t[t % T_RING][:, k, b * P:(b + 1) * P],
                                                   row[h][b][:, (2 * j + k) * P:(2 * j + k + 1) * P], ident[:])
                last.then_inc(t_made, 1)

            def times_v(i, t):
                h, j = t // STEPS, t % STEPS
                if j == 0:
                    pe.wait_ge(v_in[h], 32 * (i // GROUPS) + 32)
                    if due(i):
                        pe.wait_ge((ya_done, y_ready)[h], QB * i)
                pe.wait_ge(high_done, RS * i + (t + 1))
                for k in range(2):
                    nc.tensor.matmul(ps_oy[h][:, 0, :], v_sb[h][:, 2 * j + k, :], high[t % TRING][:, k, :],
                                     start=(j == 0 and k == 0), stop=False)
                if j % 2 == 1:
                    pe.wait_ge(low_done, RS * i + (t + 1))
                    for u in (t - 1, t):
                        for k in range(2):
                            last = nc.tensor.matmul(ps_oy[h][k * DK:(k + 1) * DK, 0, :],
                                                    vb_sb[h][:, 2 * (u % STEPS) + k, :], low[u % TRING][:, k, :],
                                                    start=False, stop=(j == STEPS - 1 and u == t))
                    last.then_inc(pv_done, 2)

            def times_wo(i, h):
                pe.wait_ge(o_copied, 2 * i + h + 1)
                for b in range(QB):
                    last = nc.tensor.matmul(ps_oy[h][:, b, :], o_sb[h][:, b * P:(b + 1) * P],
                                            wo_sb[:, bass.ds(2 * (i // GROUPS) + h, 1), :].rearrange("p a o -> p (a o)"),
                                            start=True, stop=True)
                last.then_inc(y_made, 1)

            def steps(i, n, scoring=True):
                for s in range(n):
                    for part, lag in ((times_v, PV_LAG), (turn, LAG)):
                        if s >= lag and scoring:
                            part(i, s - lag)
                        elif s < lag and due(i):
                            part(i - 1, s - lag + RS)
                    if scoring:
                        scores(i, s)
                    for h in range(2):
                        if s == OUT_AT + 1 + h * STEPS and due(i):
                            times_wo(i - 1, h)

            pe.wait_ge(wo_in, 32)
            steps(0, RS)
            steps(1, RS)
            with pe.Fori(2, ROUNDS) as i:
                steps(i, RS)
            steps(ROUNDS, DRAIN, scoring=False)

        @block.scalar
        def _(act):
            def exp_tile(i, h, b, c):
                if c == 0:
                    act.wait_ge(nmax_ready, 2 * QB * i + (h * QB + b + 1))
                tile = row[h][b][:, c * E_W:(c + 1) * E_W]
                nc.scalar.activation(tile, tile, ACT.Exp, bias=nmax[:, h, b:b + 1], scale=-1.0,
                                     accum_out=sums[:, h, b, c:c + 1]).then_inc(exp_done, 1)

            def high_part(i, t):
                act.wait_ge(t_made, RS * i + t + 1)
                if due(RS * i + t + 1 - TRING):
                    act.wait_ge(pv_done, RS * i + (t + 1 - TRING))
                nc.scalar.copy(high[t % TRING][:], ps_t[t % T_RING][:]).then_inc(high_done, 1)

            def copy_o(i, h):
                act.wait_ge(pv_done, RS * i + (h + 1) * STEPS)
                nc.scalar.copy(o_sb[h][:], ps_oy[h][:, 0, :]).then_inc(o_copied, 1)

            def scale_y(i):
                act.wait_ge(inv_done, 2 * i + 1)
                if due(i):
                    act.wait_ge(y_ready, QB * i)
                act.wait_ge(y_made, 2 * i + 1)
                for b in range(QB):
                    nc.scalar.activation(y_a[:, b, :], ps_oy[0][:, b, :], ACT.Copy,
                                         scale=rinv[:, 0, b:b + 1]).then_inc(ya_done, 1)

            def steps(i, n, scoring=True):
                for s in range(n):
                    if s >= LAG and scoring:
                        high_part(i, s - LAG)
                    elif s < LAG and due(i):
                        high_part(i - 1, s - LAG + RS)
                    for h in range(2):
                        if s == OUT_AT + h * STEPS and due(i):
                            copy_o(i - 1, h)
                    if s == OUT_AT + 2 and due(i):
                        scale_y(i - 1)
                    for u in range(2 * QB):
                        for c in range(E_ROW):
                            at = (u + 1) * S_ROW + 2 * c
                            if at == s and scoring:
                                exp_tile(i, u // QB, u % QB, c)
                            elif at == s + RS and due(i):
                                exp_tile(i - 1, u // QB, u % QB, c)

            steps(0, RS)
            steps(1, RS)
            with act.Fori(2, ROUNDS) as i:
                steps(i, RS)
            steps(ROUNDS, DRAIN, scoring=False)

        @block.vector
        def _(dve):
            def mask_tile(i, m):
                h, b, c = m // S_UNIT, m // S_ROW % QB, m % S_ROW
                if c == 0 and h == 0:
                    dve.wait_ge(mask_ready, QB * i + (b + 1))
                if due(i) and c % (E_W // S_W) == 0:
                    dve.wait_ge(t_made, RS * i + (h * STEPS + (c // 2 + 1) * (STEPS // E_ROW) - RS))
                dve.wait_ge(scored, TILES * i + (m + 1))
                dve.sem_inc(dve_held, 1)
                nc.vector.tensor_tensor_reduce(row[h][b][:, c * S_W:(c + 1) * S_W], ps_s[m % S_RING][:],
                                               mask[b][:, c * S_W:(c + 1) * S_W], 1.0, 3e38,
                                               ALU.add, ALU.min, ext[:, h, b, c:c + 1]).then_inc(masked, 1)
                if c == S_ROW - 1:
                    dve.wait_ge(masked, TILES * i + (m + 1))
                    nc.vector.tensor_reduce(nmax[:, h, b:b + 1], ext[:, h, b, :], AX.X, ALU.min)\
                        .then_inc(nmax_ready, 1)

            def low_part(i, t):
                dve.wait_ge(high_done, RS * i + (t + 1))
                nc.vector.tensor_tensor(low[t % TRING][:], ps_t[t % T_RING][:], high[t % TRING][:].bitcast(F32),
                                        ALU.subtract).then_inc(low_done, 1)

            def invert_sums(i, h):
                dve.wait_ge(exp_done, EXPS * i + (h + 1) * E_UNIT)
                nc.vector.tensor_reduce(rsum[:, h, :], sums[:, h, :, :], AX.X, ALU.add).then_inc(sum_done, 1)
                dve.wait_ge(sum_done, 2 * i + (h + 1))
                nc.vector.reciprocal(rinv[:, h, :], rsum[:, h, :]).then_inc(inv_done, 1)

            def add_y(i):
                dve.wait_ge(inv_done, 2 * i + 2)
                dve.wait_ge(ya_done, QB * i + QB)
                if due(i):
                    dve.wait_ge(y_stored, 16 * i)
                dve.wait_ge(y_made, 2 * i + 2)
                for b in range(QB):
                    nc.vector.scalar_tensor_tensor(out=y_ab[:, b, :], in0=ps_oy[1][:, b, :],
                                                   scalar=rinv[:, 1, b:b + 1], in1=y_a[:, b, :],
                                                   op0=ALU.mult, op1=ALU.add).then_inc(y_ready, 1)

            def steps(i, n, scoring=True):
                for s in range(n):
                    if scoring:
                        mask_tile(i, s)
                    if s >= LAG and scoring:
                        low_part(i, s - LAG)
                    elif s < LAG and due(i):
                        low_part(i - 1, s - LAG + RS)
                    if s == OUT_AT + 2 + STEPS and due(i):
                        add_y(i - 1)
                    if s == STEPS + S_ROW and scoring:
                        invert_sums(i, 0)
                    if s == S_ROW and due(i):
                        invert_sums(i - 1, 1)

            steps(0, RS)
            steps(1, RS)
            with dve.Fori(2, ROUNDS) as i:
                steps(i, RS)
            steps(ROUNDS, DRAIN, scoring=False)


def residual_norm(nc, x, y_scr, out):
    N, D = x.shape
    ROUNDS, QB = y_scr.shape[:2]
    GROUPS = N // (QB * P)
    PAIRS = ROUNDS // GROUPS
    W = 2
    TB = W * QB
    TILES = GROUPS // W
    with ExitStack() as ctx:
        def sb(name, shape, dt=F32):
            return ctx.enter_context(nc.sbuf_tensor(name, shape, dt))

        def sem(name):
            return ctx.enter_context(nc.semaphore(name))

        part = [[sb(f"part{u}{k}", [P, TB, D]) for k in range(PAIRS + 1)] for u in range(2)]
        stats = [sb(f"stats{u}", [P, TB, 6]) for u in range(2)]
        mv = [sb(f"mv{u}", [P, TB, 2]) for u in range(2)]
        var = [sb(f"var{u}", [P, TB]) for u in range(2)]
        std = [sb(f"std{u}", [P, TB]) for u in range(2)]
        rstd = [sb(f"rstd{u}", [P, TB]) for u in range(2)]
        normed = [sb(f"normed{u}", [P, TB, D]) for u in range(2)]
        part_in = [[sem(f"part_in{u}{k}") for k in range(PAIRS + 1)] for u in range(2)]
        dve_held = sem("norm_held")
        link = sem("link")
        var_ready = sem("var_ready")
        std_ready = sem("std_ready")
        normed_ready = sem("normed_ready")
        stored = [sem(f"out_stored{u}") for u in range(2)]
        LINKS = PAIRS + 3
        block = ctx.enter_context(nc.Block())

        @block.sync
        def _(sp):
            x_tiles = x.rearrange("(t b p) d -> t p b d", p=P, b=TB)
            y_tiles = y_scr.rearrange("(k t w) b p o -> k t p (w b) o", k=PAIRS, w=W)

            def load(t, u):
                sp.dma_start(part[u][PAIRS][:], x_tiles[t]).then_inc(part_in[u][PAIRS], 16)
                for k in range(PAIRS):
                    sp.dma_start(part[u][k][:], y_tiles[k, t]).then_inc(part_in[u][k], 16)

            for u in range(2):
                load(u, u)
            with sp.Fori(1, TILES // 2) as r:
                for u in range(2):
                    sp.wait_ge(normed_ready, 2 * r + (u - 1))
                    load(2 * r + u, u)

        @block.vector
        def _(dve):
            def tile_(r, u):
                t = 2 * r + u

                def chained(ins, k):
                    ins.then_inc(link, 1)
                    dve.wait_ge(link, LINKS * t + k + 1)

                total = part[u][PAIRS]
                dve.wait_ge(part_in[u][PAIRS], 16 * r + 16)
                for k in range(PAIRS):
                    dve.wait_ge(part_in[u][k], 16 * r + 16)
                    chained(nc.vector.tensor_tensor(total[:], total[:], part[u][k][:], ALU.add), k)
                for b in range(TB):
                    last = nc.vector.bn_stats(stats[u][:, b, :], total[:, b, :])
                last.then_inc(link, 1)
                dve.wait_ge(link, LINKS * t + PAIRS + 1)
                dve.sem_inc(dve_held, 1)
                for b in range(TB):
                    last = nc.vector.bn_aggr(mv[u][:, b, :], stats[u][:, b, :])
                chained(last, PAIRS + 1)
                nc.vector.tensor_scalar(var[u][:], mv[u][:, :, 1], EPS, None, ALU.add).then_inc(var_ready, 1)
                dve.wait_ge(std_ready, t + 1)
                chained(nc.vector.reciprocal(rstd[u][:], std[u][:]), PAIRS + 2)
                if due(r):
                    dve.wait_ge(stored[u], 16 * r)
                for b in range(TB):
                    last = nc.vector.tensor_scalar(normed[u][:, b, :], total[:, b, :], mv[u][:, b, 0:1],
                                                   rstd[u][:, b:b + 1], ALU.subtract, ALU.mult)
                last.then_inc(normed_ready, 1)

            tile_(0, 0)
            tile_(0, 1)
            with dve.Fori(1, TILES // 2) as r:
                tile_(r, 0)
                tile_(r, 1)

        @block.scalar
        def _(act):
            out_tiles = out.rearrange("(t b p) d -> t p b d", p=P, b=TB)

            def tile_(r, u):
                t = 2 * r + u
                act.wait_ge(var_ready, t + 1)
                nc.scalar.activation(std[u][:], var[u][:], ACT.Sqrt).then_inc(std_ready, 1)
                act.wait_ge(normed_ready, t + 1)
                act.dma_start(out_tiles[t], normed[u][:]).then_inc(stored[u], 16)

            tile_(0, 0)
            tile_(0, 1)
            with act.Fori(1, TILES // 2) as r:
                tile_(r, 0)
                tile_(r, 1)
            for u in range(2):
                act.wait_ge(stored[u], 16 * (TILES // 2))


def graph_attention(nc, x, adj, wk, wq, wv, wo, out):
    N, D = x.shape
    H, _, DK = wk.shape
    O = wo.shape[2]
    q_scr = nc.dram_tensor("q_scr", [H, 2, DK, N], F32).ap()
    k_scr = nc.dram_tensor("k_scr", [H, 2, DK, N], F32).ap()
    v_scr = nc.dram_tensor("v_scr", [H, P, N // P, 2 * DK], F32).ap()
    vb_scr = nc.dram_tensor("vb_scr", [H, P, N // P, DK], BF16).ap()
    y_scr = nc.dram_tensor("y_scr", [(H // 2) * (N // (2 * P)), 2, P, O], F32).ap()
    projections(nc, x, wk, wq, wv, q_scr, k_scr, v_scr, vb_scr)
    attention(nc, adj, wo, q_scr, k_scr, v_scr, vb_scr, y_scr)
    residual_norm(nc, x, y_scr, out)


_INS = ['x', 'adj', 'L0_gnn_Wks', 'L0_gnn_Wqs', 'L0_gnn_Wvs', 'L0_gnn_Wo']
_OUTS = [((4096, 256), 'float32')]


def kernel(**inputs):
    import numpy as _np
    import concourse.bacc as _bacc
    from concourse import mybir as _mybir
    from concourse.bass_utils import run_bass_kernel_spmd as _run

    nc = _bacc.Bacc("TRN2", target_bir_lowering=False, num_devices=1, dynamic_dma_scratch_size=4096)
    arrays, args = {}, []
    for name in _INS:
        a = _np.ascontiguousarray(inputs[name])
        arrays[f"in_{name}_dram"] = a
        args.append(nc.dram_tensor(f"in_{name}_dram", a.shape, _mybir.dt.from_np(a.dtype), kind="ExternalInput").ap())
    for i, (shape, dtype) in enumerate(_OUTS):
        dt = _mybir.dt.from_np(_np.dtype(dtype))
        args.append(nc.dram_tensor(f"out_{i}_dram", shape, dt, kind="ExternalOutput").ap())
    graph_attention(nc, *args)
    r = _run(nc, [arrays], core_ids=[0])
    return r.results[0]["out_0_dram"]
```

```python
from contextlib import ExitStack

import concourse.bass as bass
from concourse import mybir

ALU = mybir.AluOpType
ACT = mybir.ActivationFunctionType
AX = mybir.AxisListType
F32 = mybir.dt.float32
F32R = mybir.dt.float32r
BF16 = mybir.dt.bfloat16

P = 128
BANK = 512
BIG = 1e16
EPS = 1e-5
QB = 2
DIAG = 5


def due(n):
    return not isinstance(n, int) or n > 0


class Shared:

    def __init__(self, nc, ctx, N):
        def sb(name, shape, dt=F32):
            return ctx.enter_context(nc.sbuf_tensor(name, shape, dt))

        def sem(name):
            return ctx.enter_context(nc.semaphore(name))

        G = QB * P
        self.ident = sb("ident", [P, P])
        self.off_diag = sb("off_diag", [P, P])
        self.own = sb("own", [P, P])
        self.kept = sb("kept", [P, P])
        self.k_sb = [sb(f"k_sb{h}", [P, N], F32R) for h in range(2)]
        self.q_hl = [sb(f"q_hl{h}", [P, G], F32R) for h in range(2)]
        self.q_lh = [sb(f"q_lh{h}", [P, G], F32R) for h in range(2)]
        self.stage = [sb(f"stage{b}", [P, N]) for b in range(QB)]
        self.mask = [sb(f"mask{b}", [P, N], BF16) for b in range(QB)]
        self.qk_in = [sem(f"qk_in{h}") for h in range(2)]
        self.adj0_in = [sem(f"adj0_in{b}") for b in range(QB)]
        self.adj_in = [sem(f"adj_in{b}") for b in range(QB)]
        self.diag_done = sem("diag_done")
        self.mask_ready = sem("mask_ready")
        self.masked = sem("masked")
        self.pool_held = sem("pool_held")


def load_q(sp, sh, q_scr, p, g, h):
    DK = q_scr.shape[2] // 2
    src = q_scr[p, :, h * DK:(h + 1) * DK, bass.ts(g, QB * P)]
    for s in range(2):
        half = slice(s * DK, (s + 1) * DK)
        sp.dma_start(sh.q_hl[h][half, :].bitcast(F32), src[s]).then_inc(sh.qk_in[h], 16)
        sp.dma_start(sh.q_lh[h][half, :].bitcast(F32), src[1 - s]).then_inc(sh.qk_in[h], 16)


def make_mask(nc, pool, sh, n, g, b):
    N = sh.stage[b].shape[1]
    S_ROW = N // BANK
    if due(n):
        pool.wait_ge(sh.adj_in[b], 16 * n)
    else:
        pool.wait_ge(sh.adj0_in[b], 16 * (N // BANK))
    diag = sh.stage[b][:, bass.ds(g * QB * P + b * P, P)]
    done = DIAG * (QB * n + b)
    nc.gpsimd.tensor_copy(sh.own[:], diag).then_inc(sh.diag_done, 1)
    nc.gpsimd.tensor_tensor(sh.kept[:], diag, sh.off_diag[:], ALU.mult).then_inc(sh.diag_done, 1)
    pool.wait_ge(sh.diag_done, done + 2)
    pool.sem_inc(sh.pool_held, 1)
    nc.gpsimd.tensor_scalar(sh.own[:], sh.own[:], 1.0, None, ALU.max).then_inc(sh.diag_done, 1)
    pool.wait_ge(sh.diag_done, done + 3)
    nc.gpsimd.tensor_tensor(sh.own[:], sh.own[:], sh.ident[:], ALU.mult).then_inc(sh.diag_done, 1)
    pool.wait_ge(sh.diag_done, done + 4)
    pool.sem_inc(sh.pool_held, 1)
    nc.gpsimd.tensor_tensor(diag, sh.kept[:], sh.own[:], ALU.add).then_inc(sh.diag_done, 1)
    pool.wait_ge(sh.diag_done, done + DIAG)
    if due(n):
        pool.wait_ge(sh.masked, 2 * QB * S_ROW * (n - 1) + (QB + b + 1) * S_ROW)
    pool.sem_inc(sh.pool_held, 1)
    nc.gpsimd.tensor_scalar(sh.mask[b][:], sh.stage[b][:], -1.0, -BIG, ALU.add, ALU.mult)\
        .then_inc(sh.mask_ready, 1)


def in_turn(tiles, blocks):
    each = tiles // blocks
    return [item for b in range(blocks)
            for item in [("qk", t) for t in range(b * each, (b + 1) * each)] + [("v", b)]]


def projections(nc, sh, x, adj, wk, wq, wv, q_scr, k_scr, v_scr, vb_scr):
    N, D = x.shape
    H, _, DK = wk.shape
    CD = D // P
    CB = BANK // P
    CHUNKS = N // BANK
    PAIRS = H // 2
    TILES = 2 * PAIRS
    RING = 4
    with ExitStack() as ctx:
        def sb(name, shape, dt=F32):
            return ctx.enter_context(nc.sbuf_tensor(name, shape, dt))

        def sem(name):
            return ctx.enter_context(nc.semaphore(name))

        ident = sh.ident
        w_sb = [sb("wk_sb", [P, CD, H * DK]), sb("wq_sb", [P, CD, H * DK])]
        wv_sb = sb("wv_sb", [P, CD, H * DK])
        xin = [sb(f"xin{u}", [P, CB, D]) for u in range(2)]
        xT = [sb(f"xT{u}", [P, CD, BANK]) for u in range(2)]
        high = [sb(f"high{s}", [P, BANK], F32R) for s in range(RING)]
        low = [sb(f"low{s}", [P, BANK], F32R) for s in range(RING)]
        v_hl = [sb(f"v_hl{u}", [P, H, CB, 2, DK], F32R) for u in range(2)]
        v_bf = [sb(f"v_bf{u}", [P, H, CB, DK], BF16) for u in range(2)]
        ps_x = [ctx.enter_context(nc.psum_tensor(f"ps_x{c}", [P, BANK], F32)) for c in range(CD)]
        ps_p = [ctx.enter_context(nc.psum_tensor(f"ps_p{s}", [P, BANK], F32)) for s in range(4)]
        ps_v = [ctx.enter_context(nc.psum_tensor(f"ps_v{s}", [P, BANK], F32)) for s in range(2)]

        weights_in = [sem(f"{w}_in") for w in ("wk", "wq", "wv")]
        x_in = [sem(f"x_in{u}") for u in range(2)]
        sp_held = sem("sp_held")
        ident_zero = sem("ident_zero")
        ident_done = sem("ident_done")
        x_turned = sem("x_turned")
        xT_act = sem("xT_act")
        xT_dve = sem("xT_dve")
        projected = sem("projected")
        high_done = sem("high_done")
        low_done = sem("low_done")
        stored = [sem(f"stored{s}") for s in range(RING)]
        v_made = sem("v_made")
        v_high = sem("v_high")
        v_low = sem("v_low")
        v_stored = [sem(f"v_stored{u}") for u in range(2)]

        def stores(s, tiles):
            return sum(16 * (4 if t == 0 else 2) for t in range(s, tiles, RING))

        block = ctx.enter_context(nc.Block())

        @block.gpsimd
        def _(pool):
            xd = x.rearrange("(n b p) d -> n p b d", p=P, b=CB)
            for u in range(2):
                pool.dma_start(xin[u][:], xd[u]).then_inc(x_in[u], 16)
            nc.gpsimd.memset(ident[:], 0.0).then_inc(ident_zero, 1)
            pool.wait_ge(ident_zero, 1)
            nc.gpsimd.affine_select(out=ident[:], in_=ident[:], compare_op=ALU.not_equal, fill=1.0,
                                    base=0, pattern=[[-1, P]], channel_multiplier=1).then_inc(ident_done, 1)
            with pool.Fori(1, CHUNKS // 2) as r:
                for u in range(2):
                    pool.wait_ge(x_turned, 2 * r + (u - 1))
                    pool.dma_start(xin[u][:], xd[2 * r + u]).then_inc(x_in[u], 16)
            nc.gpsimd.tensor_scalar(sh.off_diag[:], ident[:], -1.0, 1.0, ALU.mult, ALU.add).then_inc(ident_done, 1)
            pool.wait_ge(ident_done, 2)
            for b in range(QB):
                make_mask(nc, pool, sh, 0, 0, b)

        @block.sync
        def _(sp):
            for w, t, w_in in ((wk, w_sb[0], weights_in[0]), (wq, w_sb[1], weights_in[1]),
                               (wv, wv_sb, weights_in[2])):
                for c in range(CD):
                    sp.dma_start(t[:, c, :].rearrange("p (h k) -> p h k", h=H),
                                 w[:, c * P:(c + 1) * P, :].rearrange("h p k -> p h k")).then_inc(w_in, 16)
            v_blocks = v_scr.rearrange("h p b k -> b p h k")

            def store(t, part, n, src):
                if t == 0:
                    sp.sem_inc(sp_held, 1)
                    for hh in range(2):
                        sp.dma_start(sh.k_sb[hh][part * DK:(part + 1) * DK, bass.ts(n, BANK)].bitcast(F32),
                                     src[hh * DK:(hh + 1) * DK, :].bitcast(F32)).then_inc(stored[t % RING], 16)
                else:
                    sp.dma_start((k_scr, q_scr)[t % 2][t // 2, part, :, bass.ts(n, BANK)],
                                 src[:].bitcast(F32)).then_inc(stored[t % RING], 16)

            def chunk(r, u):
                n = 2 * r + u
                for b in range(QB):
                    sp.dma_start(sh.stage[b][:, bass.ts(n, BANK)],
                                 adj[b * P:(b + 1) * P, bass.ts(n, BANK)]).then_inc(sh.adj0_in[b], 16)
                for kind, t in in_turn(TILES, CB):
                    if kind == "qk":
                        sp.wait_ge(high_done, n * TILES + (t + 1))
                        store(t, 0, n, high[t % RING])
                        sp.wait_ge(low_done, n * TILES + (t + 1))
                        store(t, 1, n, low[t % RING])
                    else:
                        sp.wait_ge(v_high, n * CB + (t + 1))
                        sp.wait_ge(v_low, n * CB + (t + 1))
                        sp.dma_start(v_blocks[n * CB + t],
                                     v_hl[u][:, :, t].rearrange("p h s k -> p h (s k)").bitcast(F32))\
                            .then_inc(v_stored[u], 16)
                sp.dma_start(vb_scr[:, :, bass.ts(n, CB), :].rearrange("h p b k -> p h b k"),
                             v_bf[u][:]).then_inc(v_stored[u], 16)

            with sp.Fori(0, CHUNKS // 2 - 1) as r:
                chunk(r, 0)
                chunk(r, 1)
            for s in range(RING):
                sp.wait_ge(stored[s], stores(s, TILES))
            for h in range(2):
                load_q(sp, sh, q_scr, 0, 0, h)
            for u in range(2):
                chunk(CHUNKS // 2 - 1, u)
            for u in range(2):
                sp.wait_ge(v_stored[u], 16 * (CB + 1) * (CHUNKS // 2))
            for s in range(RING):
                sp.wait_ge(stored[s], stores(s, TILES) * CHUNKS)
            for h in range(2):
                sp.sem_inc(sh.qk_in[h], 32)

        @block.tensor
        def _(pe):
            pe.wait_ge(ident_done, 1)

            def make_v(n, u, b, first):
                if first and b == 0:
                    pe.wait_ge(weights_in[2], 16 * CD)
                if not first or b >= 2:
                    pe.wait_ge(v_high, n * CB + (b - 1))
                    pe.wait_ge(v_low, n * CB + (b - 1))
                for c in range(CD):
                    last = nc.tensor.matmul(ps_v[b % 2][:], xT[u][:, c, b * P:(b + 1) * P],
                                            wv_sb[:, c, :], start=(c == 0), stop=(c == CD - 1))
                last.then_inc(v_made, 1)

            def turn_x(r, u):
                pe.wait_ge(x_in[u], 16 * r + 16)
                for c in range(CD):
                    for b in range(CB):
                        last = nc.tensor.transpose(ps_x[c][:, b * P:(b + 1) * P],
                                                   xin[u][:, b, c * P:(c + 1) * P], ident[:])
                last.then_inc(x_turned, 1)

            def chunk(r, u, first=False, last_chunk=False):
                n = 2 * r + u
                pe.wait_ge(xT_act, n + 1)
                pe.wait_ge(xT_dve, n + 1)
                for kind, t in in_turn(TILES, CB):
                    if kind == "v":
                        if t == CB - 1 and not last_chunk:
                            turn_x(r + u, 1 - u)
                        make_v(n, u, t, first)
                        continue
                    w = w_sb[t % 2]
                    if first and t < 2:
                        pe.wait_ge(weights_in[t], 16 * CD)
                    pair = t // 2
                    if not first or t >= 4:
                        pe.wait_ge(low_done, n * TILES + (t - 3))
                    for c in range(CD):
                        last = nc.tensor.matmul(ps_p[t % 4][:], w[:, c, pair * P:(pair + 1) * P],
                                                xT[u][:, c, :], start=(c == 0), stop=(c == CD - 1))
                    last.then_inc(projected, 1)

            turn_x(0, 0)
            chunk(0, 0, first=True)
            chunk(0, 1)
            with pe.Fori(1, CHUNKS // 2 - 1) as r:
                chunk(r, 0)
                chunk(r, 1)
            chunk(CHUNKS // 2 - 1, 0)
            chunk(CHUNKS // 2 - 1, 1, last_chunk=True)

        def heads(bank):
            return bank[:].rearrange("p (h k) -> p h k", h=H)

        @block.scalar
        def _(act):
            def copy_x(n, u):
                act.wait_ge(x_turned, n + 1)
                nc.scalar.copy(xT[u][:, 0, :], ps_x[0][:]).then_inc(xT_act, 1)

            def chunk(r, u, first=False, last_chunk=False):
                n = 2 * r + u
                if due(r):
                    act.wait_ge(v_stored[u], 16 * (CB + 1) * r)
                for kind, t in in_turn(TILES, CB):
                    if kind == "v":
                        if t == CB - 1 and not last_chunk:
                            copy_x(n + 1, 1 - u)
                        act.wait_ge(v_made, n * CB + (t + 1))
                        nc.scalar.copy(v_hl[u][:, :, t, 0, :], heads(ps_v[t % 2]))
                        nc.scalar.copy(v_bf[u][:, :, t, :], heads(ps_v[t % 2])).then_inc(v_high, 1)
                        continue
                    act.wait_ge(projected, n * TILES + (t + 1))
                    if not first or t >= RING:
                        act.wait_ge(stored[t % RING], stores(t % RING, TILES) * n + stores(t % RING, t))
                    nc.scalar.activation(high[t % RING][:], ps_p[t % 4][:], ACT.Copy,
                                         scale=(1.0, -(DK ** -0.5))[t % 2]).then_inc(high_done, 1)

            copy_x(0, 0)
            chunk(0, 0, first=True)
            chunk(0, 1)
            with act.Fori(1, CHUNKS // 2 - 1) as r:
                chunk(r, 0)
                chunk(r, 1)
            chunk(CHUNKS // 2 - 1, 0)
            chunk(CHUNKS // 2 - 1, 1, last_chunk=True)

        @block.vector
        def _(dve):
            def copy_x(n, u):
                dve.wait_ge(x_turned, n + 1)
                nc.vector.tensor_copy(xT[u][:, 1, :], ps_x[1][:]).then_inc(xT_dve, 1)

            def chunk(r, u, first=False, last_chunk=False):
                n = 2 * r + u
                for kind, t in in_turn(TILES, CB):
                    if kind == "v":
                        if t == CB - 1 and not last_chunk:
                            copy_x(n + 1, 1 - u)
                        dve.wait_ge(v_high, n * CB + (t + 1))
                        nc.vector.tensor_tensor(v_hl[u][:, :, t, 1, :], heads(ps_v[t % 2]),
                                                v_hl[u][:, :, t, 0, :].bitcast(F32), ALU.subtract).then_inc(v_low, 1)
                        continue
                    dve.wait_ge(high_done, n * TILES + (t + 1))
                    if not first or t >= RING:
                        dve.wait_ge(stored[t % RING], stores(t % RING, TILES) * n + stores(t % RING, t))
                    nc.vector.scalar_tensor_tensor(out=low[t % RING][:], in0=ps_p[t % 4][:],
                                                   scalar=(1.0, -(DK ** -0.5))[t % 2],
                                                   in1=high[t % RING][:].bitcast(F32),
                                                   op0=ALU.mult, op1=ALU.subtract).then_inc(low_done, 1)

            copy_x(0, 0)
            chunk(0, 0, first=True)
            chunk(0, 1)
            with dve.Fori(1, CHUNKS // 2 - 1) as r:
                chunk(r, 0)
                chunk(r, 1)
            chunk(CHUNKS // 2 - 1, 0)
            chunk(CHUNKS // 2 - 1, 1, last_chunk=True)


def attention(nc, sh, x, adj, wo, q_scr, k_scr, v_scr, vb_scr, y_scr, out):
    H, DK, N = v_scr.shape[0], v_scr.shape[3] // 2, x.shape[0]
    O = wo.shape[2]
    G = QB * P
    GROUPS = N // G
    PAIRS = H // 2
    ROUNDS = PAIRS * GROUPS
    S_W = BANK
    S_RING = 2
    T_RING = 4
    S_ROW = N // S_W
    S_UNIT = QB * S_ROW
    E_W = 2 * S_W
    E_ROW = N // E_W
    E_UNIT = QB * E_ROW
    STEPS = N // (2 * P)
    RS = 2 * STEPS
    LAG = STEPS + 3
    PV_LAG = LAG + 3
    TRING = 4
    TILES = 2 * S_UNIT
    EXPS = 2 * E_UNIT
    OUT_AT = PV_LAG + STEPS - RS
    SUM_AT = OUT_AT + STEPS + 6
    DRAIN = RS
    NORMED = ROUNDS - GROUPS

    ident, k_sb, q_hl, q_lh, stage, mask = sh.ident, sh.k_sb, sh.q_hl, sh.q_lh, sh.stage, sh.mask
    qk_in, adj_in, mask_ready, masked = sh.qk_in, sh.adj_in, sh.mask_ready, sh.masked
    with ExitStack() as ctx:
        def sb(name, shape, dt=F32):
            return ctx.enter_context(nc.sbuf_tensor(name, shape, dt))

        def sem(name):
            return ctx.enter_context(nc.semaphore(name))

        v_sb = [sb(f"v_sb{h}", [P, N // P, 2 * DK], F32R) for h in range(2)]
        vb_sb = [sb(f"vb_sb{h}", [P, N // P, DK], BF16) for h in range(2)]
        row = [[sb(f"row{h}{b}", [P, N]) for b in range(QB)] for h in range(2)]
        high = [sb(f"high_w{s}", [P, 2, G], F32R) for s in range(TRING)]
        low = [sb(f"low_w{s}", [P, 2, G], BF16) for s in range(TRING)]
        wo_sb = sb("wo_sb", [P, H, O])
        ext = sb("ext", [P, 2, QB, S_ROW])
        nmax = sb("nmax", [P, 2, QB])
        sums = sb("sums", [P, 2, QB, E_ROW])
        rsum = sb("rsum", [P, 2, QB])
        rinv = sb("rinv", [P, 2, QB])
        o_sb = [sb(f"o_sb{h}", [P, G]) for h in range(2)]
        y_sb = [sb(f"y_sb{h}", [P, QB, O]) for h in range(2)]
        total = sb("total", [P, QB, O])
        stats = sb("stats", [P, QB, 6])
        mean_var = sb("mean_var", [P, QB, 2])
        eps = sb("eps", [P, 1])
        std = sb("std", [P, QB])
        rstd = sb("rstd", [P, QB])
        ps_s = [ctx.enter_context(nc.psum_tensor(f"ps_s{s}", [P, S_W], F32)) for s in range(S_RING)]
        ps_t = [ctx.enter_context(nc.psum_tensor(f"ps_t{s}", [P, 2, G], F32)) for s in range(T_RING)]
        ps_oy = [ctx.enter_context(nc.psum_tensor(f"ps_oy{h}", [P, QB, O], F32)) for h in range(2)]

        dve_held = sem("dve_held")
        wo_in = sem("wo_in")
        v_in = [sem(f"v_in{h}") for h in range(2)]
        scored = sem("scored")
        nmax_ready = sem("nmax_ready")
        exp_done = sem("exp_done")
        t_made = sem("t_made")
        high_done = sem("high_w_done")
        low_done = sem("low_w_done")
        pv_done = sem("pv_done")
        o_copied = sem("o_copied")
        y_made = sem("y_made")
        sum_done = sem("sum_done")
        inv_done = sem("inv_done")
        y_scaled = [sem(f"y_scaled{h}") for h in range(2)]
        total_in = sem("total_in")
        summed = sem("summed")
        stats_done = sem("stats_done")
        moments_done = sem("moments_done")
        eps_set = sem("eps_set")
        std_ready = sem("std_ready")
        rstd_ready = sem("rstd_ready")
        normed = sem("normed")
        stored = sem("total_stored")

        block = ctx.enter_context(nc.Block())

        adj_rows = adj.rearrange("(g b p) n -> g b p n", b=QB, p=P)

        @block.sync
        def _(sp):
            def load_adj(g, b):
                sp.dma_start(stage[b][:], adj_rows[g, b]).then_inc(adj_in[b], 16)

            def load_k(p, h):
                for s in range(2):
                    sp.dma_start(k_sb[h][s * DK:(s + 1) * DK, :].bitcast(F32),
                                 k_scr[p, s, h * DK:(h + 1) * DK, :]).then_inc(qk_in[h], 16)

            def load_v(p, h):
                sp.dma_start(v_sb[h][:].bitcast(F32), v_scr[2 * p + h]).then_inc(v_in[h], 16)
                sp.dma_start(vb_sb[h][:], vb_scr[2 * p + h]).then_inc(v_in[h], 16)

            def ahead(i, p, g, new_v=False, new_k=False):
                for b in range(QB):
                    sp.wait_ge(mask_ready, QB * i + b + 1)
                    load_adj(g, b)
                for h in range(2):
                    if new_v:
                        sp.wait_ge(pv_done, RS * i - (1 - h) * STEPS)
                        load_v(p, h)
                    sp.wait_ge(scored, TILES * i + (h + 1) * S_UNIT)
                    load_q(sp, sh, q_scr, p, g, h)
                    if new_k:
                        load_k(p, h)

            for h in range(2):
                load_v(0, h)
            for h in range(2):
                sp.dma_start(wo_sb[h * DK:(h + 1) * DK], wo.rearrange("h k o -> k h o")).then_inc(wo_in, 16)

            with sp.Fori(0, GROUPS - 1) as g:
                ahead(g, 0, g + 1)
            with sp.Fori(1, PAIRS) as p:
                ahead(p * GROUPS - 1, p, 0, new_k=True)
                ahead(p * GROUPS, p, 1, new_v=True)
                with sp.Fori(1, GROUPS - 1) as g:
                    ahead(p * GROUPS + g, p, g + 1)

        @block.gpsimd
        def _(pool):
            def tiles(t):
                return t.rearrange("(g b p) o -> g p b o", b=QB, p=P)

            def load_total(m, g, before):
                if due(m):
                    pool.wait_ge(stored, 16 * m)
                    pool.sem_inc(sh.pool_held, 1)
                pool.dma_start(total[:], before[g]).then_inc(total_in, 16)

            def add_y(m):
                pool.wait_ge(total_in, 16 * m + 16)
                for h in range(2):
                    pool.wait_ge(y_scaled[h], QB * m + QB)
                    if h == 1:
                        pool.wait_ge(summed, 2 * m + 1)
                    nc.gpsimd.tensor_tensor(total[:], total[:], y_sb[h][:], ALU.add).then_inc(summed, 1)

            def store_total(m, g):
                pool.wait_ge(summed, 2 * m + 2)
                pool.sem_inc(sh.pool_held, 1)
                pool.dma_start(y_tiles[g], total[:]).then_inc(stored, 16)

            def normalise(m, g):
                pool.wait_ge(rstd_ready, m + 1 - NORMED)
                pool.sem_inc(sh.pool_held, 1)
                for b in range(QB):
                    last = nc.gpsimd.tensor_scalar(total[:, b, :], total[:, b, :], mean_var[:, b, 0:1],
                                                   rstd[:, b:b + 1], ALU.subtract, ALU.mult)
                last.then_inc(normed, 1)
                pool.wait_ge(normed, m + 1 - NORMED)
                pool.sem_inc(sh.pool_held, 1)
                pool.dma_start(tiles(out)[g], total[:]).then_inc(stored, 16)

            def output(m, g, before, last_pair=False, masks=True):
                load_total(m, g, before)
                if masks:
                    make_mask(nc, pool, sh, m + 2, (m + 2) % GROUPS, 0)
                add_y(m)
                if not last_pair:
                    store_total(m, g)
                if masks:
                    make_mask(nc, pool, sh, m + 2, (m + 2) % GROUPS, 1)

            y_tiles = y_scr.rearrange("g b p o -> g p b o")
            nc.gpsimd.memset(eps[:], EPS).then_inc(eps_set, 1)
            for b in range(QB):
                make_mask(nc, pool, sh, 1, 1, b)
            output(0, 0, tiles(x))
            with pool.Fori(1, GROUPS) as m:
                output(m, m, tiles(x))
            with pool.Fori(GROUPS, NORMED) as m:
                output(m, m % GROUPS, y_tiles)
            output(NORMED, 0, y_tiles, last_pair=True)
            with pool.Fori(NORMED + 1, ROUNDS - 2) as m:
                normalise(m - 1, m - 1 - NORMED)
                output(m, m - NORMED, y_tiles, last_pair=True)
            for m in (ROUNDS - 2, ROUNDS - 1):
                normalise(m - 1, m - 1 - NORMED)
                output(m, m - NORMED, y_tiles, last_pair=True, masks=False)
            normalise(ROUNDS - 1, GROUPS - 1)
            pool.wait_ge(stored, 16 * ROUNDS)

        @block.tensor
        def _(pe):
            def scores(i, s):
                h, j = s // STEPS, s % STEPS
                b, c = j // S_ROW, j % S_ROW
                if j == 0:
                    pe.wait_ge(qk_in[h], 64 * i + 32 * (i // GROUPS) + (64 + 32))
                if due(TILES * i + s + 1 - S_RING):
                    pe.wait_ge(masked, TILES * i + (s + 1 - S_RING))
                keys = k_sb[h][:, c * S_W:(c + 1) * S_W]
                nc.tensor.matmul(ps_s[s % S_RING][:], q_hl[h][:, b * P:(b + 1) * P], keys, start=True, stop=False)
                nc.tensor.matmul(ps_s[s % S_RING][:], q_lh[h][:, b * P:(b + 1) * P], keys, start=False, stop=True)\
                    .then_inc(scored, 1)

            def turn(i, t):
                h, j = t // STEPS, t % STEPS
                c = j // (STEPS // E_ROW)
                if j % (STEPS // E_ROW) == 0:
                    pe.wait_ge(exp_done, EXPS * i + (h * E_UNIT + E_ROW + c + 1))
                for k in range(2):
                    for b in range(QB):
                        last = nc.tensor.transpose(ps_t[t % T_RING][:, k, b * P:(b + 1) * P],
                                                   row[h][b][:, (2 * j + k) * P:(2 * j + k + 1) * P], ident[:])
                last.then_inc(t_made, 1)

            def times_v(i, t):
                h, j = t // STEPS, t % STEPS
                if j == 0:
                    pe.wait_ge(v_in[h], 32 * (i // GROUPS) + 32)
                    if due(i):
                        pe.wait_ge(y_scaled[h], QB * i)
                pe.wait_ge(high_done, RS * i + (t + 1))
                for k in range(2):
                    nc.tensor.matmul(ps_oy[h][:, 0, :], v_sb[h][:, 2 * j + k, :], high[t % TRING][:, k, :],
                                     start=(j == 0 and k == 0), stop=False)
                if j % 2 == 1:
                    pe.wait_ge(low_done, RS * i + (t + 1))
                    for u in (t - 1, t):
                        for k in range(2):
                            last = nc.tensor.matmul(ps_oy[h][k * DK:(k + 1) * DK, 0, :],
                                                    vb_sb[h][:, 2 * (u % STEPS) + k, :], low[u % TRING][:, k, :],
                                                    start=False, stop=(j == STEPS - 1 and u == t))
                    last.then_inc(pv_done, 2)

            def times_wo(i, h):
                if isinstance(i, int) and i == 0:
                    pe.wait_ge(wo_in, 32)
                pe.wait_ge(o_copied, 2 * i + h + 1)
                for b in range(QB):
                    last = nc.tensor.matmul(ps_oy[h][:, b, :], o_sb[h][:, b * P:(b + 1) * P],
                                            wo_sb[:, bass.ds(2 * (i // GROUPS) + h, 1), :].rearrange("p a o -> p (a o)"),
                                            start=True, stop=True)
                last.then_inc(y_made, 1)

            def steps(i, n, scoring=True):
                for s in range(n):
                    for part, lag in ((times_v, PV_LAG), (turn, LAG)):
                        if s >= lag and scoring:
                            part(i, s - lag)
                        elif s < lag and due(i):
                            part(i - 1, s - lag + RS)
                    if scoring:
                        scores(i, s)
                    for h in range(2):
                        if s == OUT_AT + 1 + h * STEPS and due(i):
                            times_wo(i - 1, h)

            steps(0, RS)
            steps(1, RS)
            with pe.Fori(2, ROUNDS) as i:
                steps(i, RS)
            steps(ROUNDS, DRAIN, scoring=False)

        @block.scalar
        def _(act):
            def exp_tile(i, h, b, c):
                if c == 0:
                    act.wait_ge(nmax_ready, 2 * QB * i + (h * QB + b + 1))
                tile = row[h][b][:, c * E_W:(c + 1) * E_W]
                nc.scalar.activation(tile, tile, ACT.Exp, bias=nmax[:, h, b:b + 1], scale=-1.0,
                                     accum_out=sums[:, h, b, c:c + 1]).then_inc(exp_done, 1)

            def high_part(i, t):
                act.wait_ge(t_made, RS * i + t + 1)
                if due(RS * i + t + 1 - TRING):
                    act.wait_ge(pv_done, RS * i + (t + 1 - TRING))
                nc.scalar.copy(high[t % TRING][:], ps_t[t % T_RING][:]).then_inc(high_done, 1)

            def copy_o(i, h):
                act.wait_ge(pv_done, RS * i + (h + 1) * STEPS)
                nc.scalar.copy(o_sb[h][:], ps_oy[h][:, 0, :]).then_inc(o_copied, 1)

            def scale_y(i, h):
                act.wait_ge(inv_done, 2 * i + (h + 1))
                if due(i):
                    act.wait_ge(summed, 2 * i + (h - 1))
                act.wait_ge(y_made, 2 * i + (h + 1))
                for b in range(QB):
                    nc.scalar.activation(y_sb[h][:, b, :], ps_oy[h][:, b, :], ACT.Copy,
                                         scale=rinv[:, h, b:b + 1]).then_inc(y_scaled[h], 1)

            def deviation(i):
                act.wait_ge(moments_done, i + 1 - NORMED)
                nc.scalar.activation(std[:], mean_var[:, :, 1], ACT.Sqrt, bias=eps[:]).then_inc(std_ready, 1)

            def steps(i, n, scoring=True, norming=False):
                for s in range(n):
                    if s >= LAG and scoring:
                        high_part(i, s - LAG)
                    elif s < LAG and due(i):
                        high_part(i - 1, s - LAG + RS)
                    for h in range(2):
                        if s == OUT_AT + h * STEPS and due(i):
                            copy_o(i - 1, h)
                        if s == OUT_AT + 2 + h * STEPS and due(i):
                            scale_y(i - 1, h)
                    for u in range(2 * QB):
                        for c in range(E_ROW):
                            at = (u + 1) * S_ROW + 2 * c
                            if at == s and scoring:
                                exp_tile(i, u // QB, u % QB, c)
                            elif at == s + RS and due(i):
                                exp_tile(i - 1, u // QB, u % QB, c)
                    if s == SUM_AT + 2 and norming:
                        deviation(i - 1)

            steps(0, RS)
            steps(1, RS)
            with act.Fori(2, NORMED + 1) as i:
                steps(i, RS)
            act.wait_ge(eps_set, 1)
            with act.Fori(NORMED + 1, ROUNDS) as i:
                steps(i, RS, norming=True)
            steps(ROUNDS, DRAIN, scoring=False, norming=True)

        @block.vector
        def _(dve):
            def mask_tile(i, m):
                h, b, c = m // S_UNIT, m // S_ROW % QB, m % S_ROW
                if c == 0 and h == 0:
                    dve.wait_ge(mask_ready, QB * i + (b + 1))
                if due(i) and c % (E_W // S_W) == 0:
                    dve.wait_ge(t_made, RS * i + (h * STEPS + (c // 2 + 1) * (STEPS // E_ROW) - RS))
                dve.wait_ge(scored, TILES * i + (m + 1))
                dve.sem_inc(dve_held, 1)
                nc.vector.tensor_tensor_reduce(row[h][b][:, c * S_W:(c + 1) * S_W], ps_s[m % S_RING][:],
                                               mask[b][:, c * S_W:(c + 1) * S_W], 1.0, 3e38,
                                               ALU.add, ALU.min, ext[:, h, b, c:c + 1]).then_inc(masked, 1)

            def row_extreme(i, m):
                h, b = m // S_UNIT, m // S_ROW % QB
                dve.wait_ge(masked, TILES * i + (m + 1))
                nc.vector.tensor_reduce(nmax[:, h, b:b + 1], ext[:, h, b, :], AX.X, ALU.min)\
                    .then_inc(nmax_ready, 1)

            def low_part(i, t):
                dve.wait_ge(high_done, RS * i + (t + 1))
                nc.vector.tensor_tensor(low[t % TRING][:], ps_t[t % T_RING][:], high[t % TRING][:].bitcast(F32),
                                        ALU.subtract).then_inc(low_done, 1)

            def add_sums(i, h):
                dve.wait_ge(exp_done, EXPS * i + (h + 1) * E_UNIT)
                nc.vector.tensor_reduce(rsum[:, h, :], sums[:, h, :, :], AX.X, ALU.add).then_inc(sum_done, 1)

            def invert(i, h):
                dve.wait_ge(sum_done, 2 * i + (h + 1))
                nc.vector.reciprocal(rinv[:, h, :], rsum[:, h, :]).then_inc(inv_done, 1)

            def row_stats(i):
                dve.wait_ge(summed, 2 * i + 2)
                for b in range(QB):
                    last = nc.vector.bn_stats(stats[:, b, :], total[:, b, :])
                last.then_inc(stats_done, 1)

            def moments(i):
                dve.wait_ge(stats_done, i + 1 - NORMED)
                dve.sem_inc(dve_held, 1)
                for b in range(QB):
                    last = nc.vector.bn_aggr(mean_var[:, b, :], stats[:, b, :])
                last.then_inc(moments_done, 1)

            def inverse_std(i):
                dve.wait_ge(std_ready, i + 1 - NORMED)
                nc.vector.reciprocal(rstd[:], std[:]).then_inc(rstd_ready, 1)

            def steps(i, n, scoring=True, norming=False):
                for s in range(n):
                    if scoring:
                        mask_tile(i, s)
                    if s >= LAG and scoring:
                        low_part(i, s - LAG)
                    elif s < LAG and due(i):
                        low_part(i - 1, s - LAG + RS)
                    if scoring and s % S_ROW == S_ROW - 1:
                        row_extreme(i, s)
                    if s == STEPS + S_ROW and scoring:
                        add_sums(i, 0)
                    if s == STEPS + S_ROW + 1 and scoring:
                        invert(i, 0)
                    if s == S_ROW and due(i):
                        add_sums(i - 1, 1)
                    if s == S_ROW + 1 and due(i):
                        invert(i - 1, 1)
                    for at, part in ((0, row_stats), (1, moments), (3, inverse_std)):
                        if s == SUM_AT + at and norming:
                            part(i - 1)

            steps(0, RS)
            steps(1, RS)
            with dve.Fori(2, NORMED + 1) as i:
                steps(i, RS)
            with dve.Fori(NORMED + 1, ROUNDS) as i:
                steps(i, RS, norming=True)
            steps(ROUNDS, DRAIN, scoring=False, norming=True)


def graph_attention(nc, x, adj, wk, wq, wv, wo, out):
    N, D = x.shape
    H, _, DK = wk.shape
    O = wo.shape[2]
    q_scr = nc.dram_tensor("q_scr", [H // 2, 2, 2 * DK, N], F32).ap()
    k_scr = nc.dram_tensor("k_scr", [H // 2, 2, 2 * DK, N], F32).ap()
    v_scr = nc.dram_tensor("v_scr", [H, P, N // P, 2 * DK], F32).ap()
    vb_scr = nc.dram_tensor("vb_scr", [H, P, N // P, DK], BF16).ap()
    y_scr = nc.dram_tensor("y_scr", [N // (QB * P), QB, P, O], F32).ap()
    with ExitStack() as ctx:
        sh = Shared(nc, ctx, N)
        projections(nc, sh, x, adj, wk, wq, wv, q_scr, k_scr, v_scr, vb_scr)
        attention(nc, sh, x, adj, wo, q_scr, k_scr, v_scr, vb_scr, y_scr, out)


_INS = ['x', 'adj', 'L0_gnn_Wks', 'L0_gnn_Wqs', 'L0_gnn_Wvs', 'L0_gnn_Wo']
_OUTS = [((4096, 256), 'float32')]


def kernel(**inputs):
    import numpy as _np
    import concourse.bacc as _bacc
    from concourse import mybir as _mybir
    from concourse.bass_utils import run_bass_kernel_spmd as _run

    nc = _bacc.Bacc("TRN2", target_bir_lowering=False, num_devices=1, dynamic_dma_scratch_size=4096)
    arrays, args = {}, []
    for name in _INS:
        a = _np.ascontiguousarray(inputs[name])
        arrays[f"in_{name}_dram"] = a
        args.append(nc.dram_tensor(f"in_{name}_dram", a.shape, _mybir.dt.from_np(a.dtype), kind="ExternalInput").ap())
    for i, (shape, dtype) in enumerate(_OUTS):
        dt = _mybir.dt.from_np(_np.dtype(dtype))
        args.append(nc.dram_tensor(f"out_{i}_dram", shape, dt, kind="ExternalOutput").ap())
    graph_attention(nc, *args)
    r = _run(nc, [arrays], core_ids=[0])
    return r.results[0]["out_0_dram"]
```
